# Optimizing a Trainium2 kernel written in Bass

```python
import numpy as np
import jax
import jax.numpy as jnp

def _softmax(x, axis=-1):
    return jax.nn.softmax(x, axis=axis)

def _gelu(x):
    return jax.nn.gelu(x, approximate=True)

def _silu(x):
    return jax.nn.silu(x)

def _sigmoid(x):
    return jax.nn.sigmoid(x)

def _layernorm(x, axis=-1, eps=1e-05):
    m = jnp.mean(x, axis=axis, keepdims=True)
    v = jnp.var(x, axis=axis, keepdims=True)
    return (x - m) / jnp.sqrt(v + eps)

def _scatter_add(tgt, idx, src, axis=0):
    return tgt.at[idx].add(src)

def _segment_sum(src, seg, n):
    return jax.ops.segment_sum(src, seg, n)
kernel_name = 'mk_vit_tower_d1_tok_img256_r4_a9f777'

def setup_inputs(seed: int=0):
    np.random.seed(seed)
    _w = jnp.asarray

    def _rec_inputs():
        import jax
        import jax.numpy as jnp
        _rk = jax.random.key(seed)
        x = -0.000392918 + 0.999932 * jax.random.normal(jax.random.fold_in(_rk, 1), (16, 1, 128, 512), jnp.float32)
        return x
    x = _rec_inputs()

    def _L0_tok_setup():
        import jax, jax.numpy as jnp
        import numpy as np
        PATCH = 8
        EMBED = 64
        N_MELS = 128
        N_FRAMES = 512
        BATCH = 64
        NUM_PATCHES = N_MELS // PATCH * (N_FRAMES // PATCH)
        key = jax.random.key(seed)
        k1, k2, k3, k4 = jax.random.split(key, 4)
        x = jax.random.normal(k1, (BATCH, 1, N_MELS, N_FRAMES), dtype=jnp.float32)
        W = jax.random.normal(k2, (EMBED, PATCH * PATCH), dtype=jnp.float32) * (1.0 / np.sqrt(PATCH * PATCH))
        b = jax.random.normal(k3, (EMBED,), dtype=jnp.float32) * 0.01
        pos_embed = jax.random.normal(k4, (1, NUM_PATCHES, EMBED), dtype=jnp.float32) * 0.02
        return {'x': x, 'W': W, 'b': b, 'pos_embed': pos_embed}
    _L0_tok_all = _L0_tok_setup()
    _L0_tok_in = {k: v for k, v in _L0_tok_all.items() if k in ('W', 'b', 'pos_embed')}
    del _L0_tok_all

    def _L0_attn_setup():
        import jax, jax.numpy as jnp
        import numpy as np
        HEADS = 8
        EPS = 1e-05

        def _ln(t, w, b, headc):
            m = jnp.mean(t, axis=-1, keepdims=True)
            d = t - m
            std = jnp.sqrt(jnp.sum(d * d, axis=-1, keepdims=True) / (headc - 1))
            return w * (d / (std + EPS)) + b
        key = jax.random.key(seed)
        B, N, C = (32, 1024, 64)
        headc = C // HEADS
        x = jax.random.normal(key, (B, N, C), dtype=jnp.float32)
        return {'x': x, 'kln_weight': jnp.ones((HEADS, 1, headc), dtype=jnp.float32), 'kln_bias': jnp.zeros((HEADS, 1, headc), dtype=jnp.float32), 'vln_weight': jnp.ones((HEADS, 1, headc), dtype=jnp.float32), 'vln_bias': jnp.zeros((HEADS, 1, headc), dtype=jnp.float32)}
    _L0_attn_all = _L0_attn_setup()
    _L0_attn_in = {k: v for k, v in _L0_attn_all.items() if k in ('kln_weight', 'kln_bias', 'vln_weight', 'vln_bias')}
    del _L0_attn_all

    def _L0_ffn_setup():
        import jax, jax.numpy as jnp
        import numpy as np
        B, S, H, F, E, K = (8, 1024, 64, 128, 16, 2)
        EPS = 1e-05
        key = jax.random.key(seed)
        ks = jax.random.split(key, 9)
        sc = 0.02
        return {'x': jax.random.normal(ks[0], (B, S, H), dtype=jnp.float32), 'gate_w': jax.random.normal(ks[1], (H, E), dtype=jnp.float32) * sc, 'gate_b': jnp.zeros((E,), dtype=jnp.float32), 'w1': jax.random.normal(ks[2], (E, H, F), dtype=jnp.float32) * sc, 'b1': jnp.zeros((E, F), dtype=jnp.float32), 'w2': jax.random.normal(ks[3], (E, F, H), dtype=jnp.float32) * sc, 'b2': jnp.zeros((E, H), dtype=jnp.float32), 'gamma': jnp.ones((H,), dtype=jnp.float32), 'beta': jnp.zeros((H,), dtype=jnp.float32)}
    _L0_ffn_all = _L0_ffn_setup()
    _L0_ffn_in = {k: v for k, v in _L0_ffn_all.items() if k in ('gate_w', 'gate_b', 'w1', 'b1', 'w2', 'b2', 'gamma', 'beta')}
    del _L0_ffn_all
    return {'x': x, 'L0_tok_W': _L0_tok_in['W'], 'L0_tok_b': _L0_tok_in['b'], 'L0_tok_pos_embed': _L0_tok_in['pos_embed'], 'L0_attn_kln_weight': _L0_attn_in['kln_weight'], 'L0_attn_kln_bias': _L0_attn_in['kln_bias'], 'L0_attn_vln_weight': _L0_attn_in['vln_weight'], 'L0_attn_vln_bias': _L0_attn_in['vln_bias'], 'L0_ffn_gate_w': _L0_ffn_in['gate_w'], 'L0_ffn_gate_b': _L0_ffn_in['gate_b'], 'L0_ffn_w1': _L0_ffn_in['w1'], 'L0_ffn_b1': _L0_ffn_in['b1'], 'L0_ffn_w2': _L0_ffn_in['w2'], 'L0_ffn_b2': _L0_ffn_in['b2'], 'L0_ffn_gamma': _L0_ffn_in['gamma'], 'L0_ffn_beta': _L0_ffn_in['beta']}

def reference(x, L0_tok_W, L0_tok_b, L0_tok_pos_embed, L0_attn_kln_weight, L0_attn_kln_bias, L0_attn_vln_weight, L0_attn_vln_bias, L0_ffn_gate_w, L0_ffn_gate_b, L0_ffn_w1, L0_ffn_b1, L0_ffn_w2, L0_ffn_b2, L0_ffn_gamma, L0_ffn_beta):
    import jax
    import jax.numpy as jnp

    def _L0_tok_ref(x, W, b, pos_embed):
        import jax, jax.numpy as jnp
        import numpy as np
        PATCH = 8
        EMBED = 64
        N_MELS = 128
        N_FRAMES = 512
        BATCH = 64
        NUM_PATCHES = N_MELS // PATCH * (N_FRAMES // PATCH)
        B = x.shape[0]
        mp, fp = (N_MELS // PATCH, N_FRAMES // PATCH)
        xs = x[:, 0]
        patches = xs.reshape(B, mp, PATCH, fp, PATCH).transpose(0, 1, 3, 2, 4).reshape(B, mp * fp, PATCH * PATCH)
        emb = jnp.einsum('bnk,ek->bne', patches, W) + b
        return emb + pos_embed

    def _L0_attn_ref(x, kln_weight, kln_bias, vln_weight, vln_bias):
        import jax, jax.numpy as jnp
        import numpy as np
        HEADS = 8
        EPS = 1e-05

        def _ln(t, w, b, headc):
            m = jnp.mean(t, axis=-1, keepdims=True)
            d = t - m
            std = jnp.sqrt(jnp.sum(d * d, axis=-1, keepdims=True) / (headc - 1))
            return w * (d / (std + EPS)) + b
        B, N, C = x.shape
        headc = C // HEADS
        qkv = x.reshape(B, N, HEADS, headc).transpose(0, 2, 1, 3)
        k = _ln(qkv, kln_weight, kln_bias, headc)
        v = _ln(qkv, vln_weight, vln_bias, headc)
        kv = jnp.einsum('bhnd,bhne->bhde', k, v) / N
        out = jnp.einsum('bhnd,bhde->bhne', qkv, kv)
        out = out.transpose(0, 2, 1, 3).reshape(B, N, C)
        return out + x

    def _L0_ffn_ref(x, gate_w, gate_b, w1, b1, w2, b2, gamma, beta):
        import jax, jax.numpy as jnp
        import numpy as np
        B, S, H, F, E, K = (8, 1024, 64, 128, 16, 2)
        EPS = 1e-05
        gate_logits = x @ gate_w + gate_b
        topk_vals, topk_idx = jax.lax.top_k(gate_logits, K)
        topk_w = jax.nn.softmax(topk_vals, axis=-1)
        h = jax.nn.relu(jnp.einsum('bsh,ehf->bsef', x, w1) + b1)
        expert_out = jnp.einsum('bsef,efh->bseh', h, w2) + b2
        sel = jnp.take_along_axis(expert_out, topk_idx[:, :, :, None], axis=2)
        moe = jnp.sum(topk_w[..., None] * sel, axis=2)
        y = x + moe
        mu = jnp.mean(y, axis=-1, keepdims=True)
        var = jnp.var(y, axis=-1, keepdims=True)
        return (y - mu) / jnp.sqrt(var + EPS) * gamma + beta
    h = _L0_tok_ref(x, L0_tok_W, L0_tok_b, L0_tok_pos_embed)
    h = h + _L0_attn_ref(_layernorm(h, axis=-1), L0_attn_kln_weight, L0_attn_kln_bias, L0_attn_vln_weight, L0_attn_vln_bias)
    h = h + _L0_ffn_ref(_layernorm(h, axis=-1), L0_ffn_gate_w, L0_ffn_gate_b, L0_ffn_w1, L0_ffn_b1, L0_ffn_w2, L0_ffn_b2, L0_ffn_gamma, L0_ffn_beta)
    return h

_drawn_inputs = setup_inputs


def setup_inputs(seed=0):
    import zlib

    import numpy as np

    out = dict(_drawn_inputs(seed))
    spreads = {'L0_attn_kln_weight': (1.0, 0.2),
     'L0_attn_kln_bias': (0.0, 0.752),
     'L0_attn_vln_weight': (1.0, 0.2),
     'L0_attn_vln_bias': (0.0, 0.768),
     'L0_ffn_gate_b': (0.0, 0.462),
     'L0_ffn_b1': (0.0, 0.8),
     'L0_ffn_b2': (0.0, 0.474),
     'L0_ffn_gamma': (1.0, 0.2),
     'L0_ffn_beta': (0.0, 0.312)}
    factors = {'L0_tok_b': 6.015,
     'L0_tok_pos_embed': 2.924,
     'L0_ffn_gate_w': 3.524,
     'L0_ffn_w1': 8.0,
     'L0_ffn_w2': 8.0}
    for name, (base, spread) in spreads.items():
        noise = np.random.default_rng([zlib.crc32(name.encode()), seed]).standard_normal(out[name].shape)
        drawn = base * np.exp(spread * noise) if base else spread * noise
        out[name] = jnp.asarray(drawn.astype(out[name].dtype))
    for name, factor in factors.items():
        out[name] = (out[name] * factor).astype(out[name].dtype)
    return out
```

```python
from contextlib import ExitStack

import concourse.bass as bass
from concourse import mybir

F32 = mybir.dt.float32
F32R = mybir.dt.float32r
U32 = mybir.dt.uint32
ALU = mybir.AluOpType
ACT = mybir.ActivationFunctionType
AX_X = mybir.AxisListType.X

P = 128
B = 16
N = 1024
T = N // P
C = 64
HEADS = 8
HD = C // HEADS
GROUPS = T * HEADS
NE = 16
FH = 128
UN = P // NE
CHUNKS = FH // UN
W = 512
TILES = N // W
TT = W // P
SLOTS = CHUNKS * TILES // 2
SRING = 4
GRING = 8
LAG = 2
EPS = 1e-5
DVE_STEP = SLOTS // 2 * 3
POOL_STEP = SLOTS // 2


def on_pool(slot, half):
    return slot % 2 == 1 and half == 1


def dve_gated(slot):
    return slot // 2 * 3 + (3 if slot % 2 else 2)


def pool_gated(slot):
    return (slot + 1) // 2


def tower(nc, patches, tok_w, tok_b, pos, k_w, k_b, v_w, v_b, gate_w, gate_b, w1, b1, w2, b2,
          gamma, beta, ident, head_mask, numbers, out):
    with ExitStack() as ctx:
        def sb(name, shape, dt=F32):
            return ctx.enter_context(nc.sbuf_tensor(name, shape, dt))

        def sem(name):
            return ctx.enter_context(nc.semaphore(name))

        eye = sb("eye", [P, P])
        eye2 = sb("eye2", [P, C])
        mask_n = sb("mask_n", [C, C])
        expert_no = sb("expert_no", [P, NE])
        euler = sb("euler", [P, T])
        wt = sb("wt", [C, C])
        posb = sb("posb", [P, T * C])
        tokb = sb("tokb", [P, C])
        kaug = sb("kaug", [C + 1, C])
        vaug = sb("vaug", [C + 1, C])
        kwv = sb("kwv", [C, 2])
        gw2 = sb("gw2", [P, NE])
        gbias = sb("gbias", [P, NE])
        w1f = sb("w1f", [P, CHUNKS * P])
        w1h = sb("w1h", [P, CHUNKS * P], F32R)
        w1l = sb("w1l", [P, CHUNKS * P], F32R)
        w2s = sb("w2s", [P, CHUNKS * C])
        b1s = sb("b1s", [P, CHUNKS])
        b2x = sb("b2x", [P, C])
        gam = sb("gam", [P, C])
        bet = sb("bet", [P, C])
        epsc = sb("epsc", [P, 1])
        xin = [sb(f"xin{i}", [C, N]) for i in range(2)]
        h = [sb(f"h{i}", [P, T * C]) for i in range(2)]
        rstd1 = [sb(f"rstd1{i}", [P, T]) for i in range(2)]
        hsum = sb("hsum", [P, GROUPS])
        hmean = sb("hmean", [P, GROUPS])
        sum1 = sb("sum1", [P, T])
        mean1 = sb("mean1", [P, T])
        off = sb("off", [P, GROUPS])
        off2 = sb("off2", [P, GROUPS])
        hc = sb("hc", [P, T * C])
        sq1 = sb("sq1", [P, T * C])
        hss = sb("hss", [P, GROUPS])
        tss = sb("tss", [P, GROUPS])
        ss1 = sb("ss1", [P, T])
        std1 = sb("std1", [P, T])
        hstd = sb("hstd", [P, GROUPS])
        den = sb("den", [P, GROUPS])
        den2 = sb("den2", [P, GROUPS])
        rden = sb("rden", [P, GROUPS])
        fac = sb("fac", [P, GROUPS])
        naug = sb("naug", [P, T, C + 1])
        hcen = sb("hcen", [P, T * C])
        ht = sb("ht", [C, N])
        maug = sb("maug", [C + 1, C + 1])
        tm = sb("tm", [C + 1, C])
        am0 = sb("am0", [C, C])
        am = sb("am", [C, C])
        osc = sb("osc", [P, T * C])
        h2 = sb("h2", [P, T * C])
        sum2 = sb("sum2", [P, T])
        mean2 = sb("mean2", [P, T])
        cen2 = sb("cen2", [P, T * C])
        sq2 = sb("sq2", [P, T * C])
        ss2 = sb("ss2", [P, T])
        std2 = sb("std2", [P, T])
        rstd2 = sb("rstd2", [P, T])
        xn = [sb(f"xn{i}", [P, T * C]) for i in range(2)]
        hb = [sb(f"hb{i}", [P, T * C]) for i in range(2)]
        xs = [sb(f"xs{i}", [P, N], F32R) for i in range(2)]
        logit = sb("logit", [P, T * NE])
        top = sb("top", [P, T, 8])
        topi = sb("topi", [P, T, 8], U32)
        topf = sb("topf", [P, T, 2])
        gap = sb("gap", [P, T])
        egap = sb("egap", [P, T])
        gden = sb("gden", [P, T])
        wt1 = sb("wt1", [P, T])
        wt2 = sb("wt2", [P, T])
        hit1 = sb("hit1", [P, T * NE])
        hit2 = sb("hit2", [P, T * NE])
        gat1 = sb("gat1", [P, T * NE])
        gat2 = sb("gat2", [P, T * NE])
        gates = sb("gates", [P, T * NE])
        spread = sb("spread", [P, N])
        gt = [sb(f"gt{i}", [P, N]) for i in range(2)]
        rl = [sb(f"rl{i}", [P, W]) for i in range(2)]
        hg = [sb(f"hg{i}", [P, W]) for i in range(GRING)]
        yt = [sb(f"yt{i}", [P, W]) for i in range(TILES)]
        ysum = sb("ysum", [P, T * C])
        sum3 = sb("sum3", [P, T])
        mean3 = sb("mean3", [P, T])
        cen3 = sb("cen3", [P, T * C])
        sq3 = sb("sq3", [P, T * C])
        ss3 = sb("ss3", [P, T])
        std3 = sb("std3", [P, T])
        rstd3 = sb("rstd3", [P, T])
        yn = sb("yn", [P, T * C])
        yg = sb("yg", [P, T * C])
        res = sb("res", [P, T * C])

        ps = [ctx.enter_context(nc.psum_tensor(f"ps{i}", [P, W], F32)) for i in range(SRING)]
        py = ctx.enter_context(nc.psum_tensor("py", [P, W], F32))
        pf = ctx.enter_context(nc.psum_tensor("pf", [P, W], F32))
        pa = ctx.enter_context(nc.psum_tensor("pa", [P, W], F32))
        pb = ctx.enter_context(nc.psum_tensor("pb", [P, W], F32))

        const_in = sem("const_in")
        b2_in = sem("b2_in")
        w1_split, weights_ready, ones_ready, zero_ready = (
            sem(x) for x in ("w1_split", "weights_ready", "ones_ready", "zero_ready"))
        loaded, stored = sem("loaded"), sem("stored")
        embedded, h_ready, sums_ready, hmean_ready, mean1_ready, off_ready, off2_ready = (
            sem(x) for x in ("embedded", "h_ready", "sums_ready", "hmean_ready", "mean1_ready",
                             "off_ready", "off2_ready"))
        sum1_ready, hc_ready, sq1_ready, hss_ready, tss_ready, ss1_ready, std1_ready, hstd_ready = (
            sem(x) for x in ("sum1_ready", "hc_ready", "sq1_ready", "hss_ready", "tss_ready",
                             "ss1_ready", "std1_ready", "hstd_ready"))
        rstd1_ready, den_ready, den2_ready, rden_ready, fac_ready, n_ready, hcen_ready = (
            sem(x) for x in ("rstd1_ready", "den_ready", "den2_ready", "rden_ready", "fac_ready",
                             "n_ready", "hcen_ready"))
        ht_turned, ht_copied = sem("ht_turned"), sem("ht_copied")
        m_done, m_copied, t_done, t_copied, kv_done, am0_ready, am_ready = (
            sem(x) for x in ("m_done", "m_copied", "t_done", "t_copied", "kv_done", "am0_ready",
                             "am_ready"))
        attended, osc_ready, h2_ready, sum2_ready, mean2_ready, cen2_ready, sq2_ready = (
            sem(x) for x in ("attended", "osc_ready", "h2_ready", "sum2_ready", "mean2_ready",
                             "cen2_ready", "sq2_ready"))
        ss2_ready, std2_ready, rstd2_ready, xn_ready, hb_ready = (
            sem(x) for x in ("ss2_ready", "std2_ready", "rstd2_ready", "xn_ready", "hb_ready"))
        x_turned, hi_ready, lo_ready = sem("x_turned"), sem("hi_ready"), sem("lo_ready")
        logits_done, logit_ready, top_ready, topi_ready, topf_ready, gap_ready, egap_ready = (
            sem(x) for x in ("logits_done", "logit_ready", "top_ready", "topi_ready", "topf_ready",
                             "gap_ready", "egap_ready"))
        gden_ready, wt1_ready, wt2_ready, hits_ready, gats_ready, gates_ready = (
            sem(x) for x in ("gden_ready", "wt1_ready", "wt2_ready", "hits_ready", "gats_ready",
                             "gates_ready"))
        spread_ready = sem("spread_ready")
        g_turned, g_copied = sem("g_turned"), sem("g_copied")
        s_done, relu_done = sem("s_done"), sem("relu_done")
        gated_dve, gated_pool = sem("gated_dve"), sem("gated_pool")
        y_chunks, y_copied, f_done = sem("y_chunks"), sem("y_copied"), sem("f_done")
        passed = {e: sem(f"passed_{e}") for e in ("pe", "dve", "sp")}
        ysum_ready, sum3_ready, mean3_ready, cen3_ready, sq3_ready, ss3_ready, std3_ready = (
            sem(x) for x in ("ysum_ready", "sum3_ready", "mean3_ready", "cen3_ready", "sq3_ready",
                             "ss3_ready", "std3_ready"))
        rstd3_ready, yn_ready, yg_ready, res_ready = (
            sem(x) for x in ("rstd3_ready", "yn_ready", "yg_ready", "res_ready"))

        def wait(eng, s, value):
            if not isinstance(value, int) or value > 0:
                eng.wait_ge(s, value)

        def settle(eng, name):
            eng.sem_inc(passed[name], 1)

        def blocks(buf):
            return buf[:, :].rearrange("p (t c) -> p t c", t=T)

        def heads(buf):
            return buf[:, :].rearrange("p (g d) -> p g d", d=HD)

        def per_block(small, n=C):
            return small[:, :].unsqueeze(2).to_broadcast([P, T, n])

        def per_head(small):
            return small[:, :].unsqueeze(2).to_broadcast([P, GROUPS, HD])

        def over_blocks(row, n=C):
            return row[:, :].unsqueeze(1).to_broadcast([P, T, n])

        CONSTS = [
            (eye[:, :], ident[:, :]), (eye2[0:C, :], ident[0:C, 0:C]), (eye2[C:P, :], ident[0:C, 0:C]),
            (mask_n[:, :], head_mask[:, :]), (expert_no[:, :], numbers[:, 0:NE]),
            (euler[:, :], numbers[:, NE:NE + T]), (wt[:, :], tok_w[:, :]), (posb[:, :], pos[:, :]),
            (tokb[:, :], tok_b.unsqueeze(0).to_broadcast([P, C])),
            (kwv[:, 0:1], k_w.unsqueeze(1)), (kwv[:, 1:2], v_w.unsqueeze(1)),
            (kaug[C:C + 1, :], k_b.unsqueeze(0)), (vaug[C:C + 1, :], v_b.unsqueeze(0)),
            (gw2[0:C, :], gate_w[:, :]), (gw2[C:P, :], gate_w[:, :]),
            (gbias[:, :], gate_b.unsqueeze(0).to_broadcast([P, NE])),
            (w1f[0:C, :], w1[:, :]), (w1f[C:P, :], w1[:, :]), (w2s[:, :], w2[:, :]),
            (b1s[:, :], b1[:, :]),
            (gam[:, :], gamma.unsqueeze(0).to_broadcast([P, C])),
            (bet[:, :], beta.unsqueeze(0).to_broadcast([P, C])),
        ]
        ALL_CONSTS = 16 * len(CONSTS)

        def pipeline(eng, embed, attend, step):
            embed(0, 0)
            attend(0, 0)
            embed(1, 1)
            step(0, 0, first=True)
            step(1, 1)
            with eng.Fori(0, (B - 4) // 2) as i:
                step(2 * i + 2, 0)
                step(2 * i + 3, 1)
            step(B - 2, 0, embeds=False)
            step(B - 1, 1, embeds=False, attends=False)
            step(B, 0, embeds=False, attends=False, feeds=False)

        block = ctx.enter_context(nc.Block())

        @block.sync
        def _(sp):
            for dst, src in CONSTS[:len(CONSTS) // 2]:
                sp.dma_start(dst, src).then_inc(const_in, 16)

            def load(k, par):
                wait(sp, loaded, 16 * k)
                settle(sp, "sp")
                wait(sp, embedded, k - 1)
                settle(sp, "sp")
                sp.dma_start(xin[par][:, :], patches[k, :, :] if isinstance(k, int)
                             else patches[bass.ds(k, 1), :, :].rearrange("a c n -> (a c) n")).then_inc(loaded, 16)

            def store(k):
                wait(sp, stored, 16 * k)
                settle(sp, "sp")
                sp.wait_ge(res_ready, k + 1)
                settle(sp, "sp")
                dst = out[k, :, :] if isinstance(k, int) else \
                    out[bass.ds(k, 1), :, :].rearrange("a p n -> (a p) n")
                sp.dma_start(dst, res[:, :]).then_inc(stored, 16)

            def step(s, par, first=False, embeds=True, attends=True, feeds=True):
                if embeds:
                    load(s + 2, par)
                if not first:
                    store(s - 1)

            load(0, 0)
            load(1, 1)
            pipeline(sp, lambda k, par: None, lambda k, par: None, step)
            sp.wait_ge(stored, 16 * B)

        @block.gpsimd
        def _(pool):
            nc.gpsimd.memset(b2x[:, :], 0.0).then_inc(zero_ready, 1)
            nc.gpsimd.memset(naug[:, :, C:C + 1], 1.0).then_inc(ones_ready, 1)
            nc.gpsimd.memset(epsc[:, :], EPS).then_inc(ones_ready, 1)
            pool.wait_ge(zero_ready, 1)
            pool.dma_start(b2x[0:P:UN, :], b2[:, :]).then_inc(b2_in, 16)
            pool.wait_ge(const_in, ALL_CONSTS)

            def center_tokens(k, par):
                pool.wait_ge(mean1_ready, k + 1)
                wait(pool, ht_turned, 2 * k)
                nc.gpsimd.tensor_tensor(blocks(hcen), blocks(h[par]), per_block(mean1),
                                        ALU.subtract).then_inc(hcen_ready, 1)

            def add_attention(k, par):
                pool.wait_ge(osc_ready, k + 1)
                wait(pool, hb_ready, k)
                nc.gpsimd.tensor_tensor(h2[:, :], osc[:, :], h[par][:, :], ALU.add).then_inc(h2_ready, 1)

            def center_again(k):
                pool.wait_ge(mean2_ready, k + 1)
                pool.wait_ge(h2_ready, k + 1)
                wait(pool, sq2_ready, k)
                nc.gpsimd.tensor_tensor(blocks(cen2), blocks(h2), per_block(mean2),
                                        ALU.subtract).then_inc(cen2_ready, 1)

            def scale_again(k, par):
                pool.wait_ge(rstd2_ready, k + 1)
                pool.wait_ge(cen2_ready, k + 1)
                wait(pool, ysum_ready, k - 1)
                nc.gpsimd.tensor_tensor(blocks(xn[par]), blocks(cen2), per_block(rstd2),
                                        ALU.mult).then_inc(xn_ready, 1)

            def exp_gap(k):
                pool.wait_ge(gap_ready, k + 1)
                wait(pool, wt2_ready, k)
                nc.gpsimd.tensor_tensor(egap[:, :], euler[:, :], gap[:, :], ALU.pow).then_inc(egap_ready, 1)

            def add_beta(k, par):
                pool.wait_ge(h2_ready, k + 1)
                wait(pool, res_ready, k - 1)
                nc.gpsimd.tensor_tensor(blocks(hb[par]), blocks(h2), over_blocks(bet),
                                        ALU.add).then_inc(hb_ready, 1)

            def center_last(k):
                pool.wait_ge(mean3_ready, k + 1)
                wait(pool, yn_ready, k)
                nc.gpsimd.tensor_tensor(blocks(cen3), blocks(ysum), per_block(mean3),
                                        ALU.subtract).then_inc(cen3_ready, 1)

            def times_gamma(k):
                pool.wait_ge(yn_ready, k + 1)
                nc.gpsimd.tensor_tensor(blocks(yg), blocks(yn), over_blocks(gam),
                                        ALU.mult).then_inc(yg_ready, 1)

            def add_residual(k, par):
                pool.wait_ge(yg_ready, k + 1)
                wait(pool, stored, 16 * k)
                nc.gpsimd.tensor_tensor(res[:, :], yg[:, :], hb[par][:, :], ALU.add).then_inc(res_ready, 1)

            def gate_chunk(s, par, j):
                chunk = 2 * j + 1
                pool.wait_ge(relu_done, 32 * s + chunk + 1)
                wait(pool, y_chunks, SLOTS * s + j - GRING // 2 + 1)
                cols = slice(j // (SLOTS // TILES) * W, (j // (SLOTS // TILES) + 1) * W)
                nc.gpsimd.tensor_tensor(hg[chunk % GRING][:, :], rl[j // 2 % 2][:, :], gt[par][:, cols],
                                        ALU.mult).then_inc(gated_pool, 1)

            def embed(k, par):
                center_tokens(k, par)

            def attend(k, par):
                add_attention(k, par)
                center_again(k)
                scale_again(k, par)
                exp_gap(k)
                add_beta(k, par)

            def step(s, par, first=False, embeds=True, attends=True, feeds=True):
                for j in range(SLOTS):
                    if feeds and on_pool(j, 1):
                        gate_chunk(s, par, j)
                    if embeds and j == 1:
                        center_tokens(s + 2, par)
                    if attends and j == 2:
                        add_attention(s + 1, 1 - par)
                    if attends and j == 4:
                        center_again(s + 1)
                    if attends and j == 6:
                        scale_again(s + 1, 1 - par)
                    if not first and j == 7:
                        center_last(s - 1)
                    if attends and j == 10:
                        exp_gap(s + 1)
                    if not first and j == 11:
                        times_gamma(s - 1)
                    if not first and j == 12:
                        add_residual(s - 1, 1 - par)
                    if attends and j == 14:
                        add_beta(s + 1, 1 - par)

            pipeline(pool, embed, attend, step)

        @block.scalar
        def _(act):
            for dst, src in CONSTS[len(CONSTS) // 2:]:
                act.dma_start(dst, src).then_inc(const_in, 16)
            act.wait_ge(const_in, ALL_CONSTS)
            act.wait_ge(ones_ready, 2)
            nc.scalar.activation(w1h[:, :], w1f[:, :], ACT.Copy).then_inc(w1_split, 1)

            def square_heads(k):
                act.wait_ge(hc_ready, k + 1)
                wait(act, hss_ready, k)
                nc.scalar.activation(sq1[:, :], hc[:, :], ACT.Square).then_inc(sq1_ready, 1)

            def roots(k):
                act.wait_ge(ss1_ready, k + 1)
                nc.scalar.activation(std1[:, :], ss1[:, :], ACT.Sqrt, bias=epsc[:, 0:1],
                                     scale=1.0 / C).then_inc(std1_ready, 1)
                nc.scalar.activation(hstd[:, :], hss[:, :], ACT.Sqrt,
                                     scale=1.0 / (HD - 1)).then_inc(hstd_ready, 1)

            def copy_ht(k, half):
                act.wait_ge(ht_turned, 2 * k + half + 1)
                wait(act, attended, k)
                nc.scalar.activation(ht[:, half * W:(half + 1) * W], pa[0:C, :],
                                     ACT.Copy).then_inc(ht_copied, 1)

            def copy_t(k):
                act.wait_ge(t_done, k + 1)
                nc.scalar.activation(tm[:, :], pa[0:C + 1, 128:128 + C], ACT.Copy).then_inc(t_copied, 1)

            def square_again(k):
                act.wait_ge(cen2_ready, k + 1)
                wait(act, ss2_ready, k)
                nc.scalar.activation(sq2[:, :], cen2[:, :], ACT.Square).then_inc(sq2_ready, 1)

            def root_again(k):
                act.wait_ge(ss2_ready, k + 1)
                nc.scalar.activation(std2[:, :], ss2[:, :], ACT.Sqrt, bias=epsc[:, 0:1],
                                     scale=1.0 / C).then_inc(std2_ready, 1)

            def round_hi(k, par, half):
                act.wait_ge(x_turned, 2 * k + half + 1)
                nc.scalar.activation(xs[par][0:C, half * W:(half + 1) * W], pb[0:C, :],
                                     ACT.Copy).then_inc(hi_ready, 1)

            def spread_gates(k):
                act.wait_ge(gates_ready, k + 1)
                wait(act, g_turned, 2 * k)
                nc.scalar.activation(spread[:, :].rearrange("p (g u) -> p g u", u=UN),
                                     gates[:, :].unsqueeze(2).to_broadcast([P, T * NE, UN]),
                                     ACT.Copy).then_inc(spread_ready, 1)

            def copy_gates(k, par, half):
                act.wait_ge(g_turned, 2 * k + half + 1)
                wait(act, f_done, 2 * (k - 1))
                nc.scalar.activation(gt[par][:, half * W:(half + 1) * W], pb[:, :],
                                     ACT.Copy).then_inc(g_copied, 1)

            def copy_y(k, tile):
                act.wait_ge(y_chunks, SLOTS * k + SLOTS // TILES * (tile + 1))
                wait(act, f_done, TILES * (k - 1) + tile + 1)
                nc.scalar.activation(yt[tile][:, :], py[:, :], ACT.Copy).then_inc(y_copied, 1)

            def square_last(k):
                act.wait_ge(cen3_ready, k + 1)
                wait(act, ss3_ready, k)
                nc.scalar.activation(sq3[:, :], cen3[:, :], ACT.Square).then_inc(sq3_ready, 1)

            def root_last(k):
                act.wait_ge(ss3_ready, k + 1)
                nc.scalar.activation(std3[:, :], ss3[:, :], ACT.Sqrt, bias=epsc[:, 0:1],
                                     scale=1.0 / C).then_inc(std3_ready, 1)

            def relu_slot(s, j):
                for half in range(2):
                    chunk = 2 * j + half
                    act.wait_ge(s_done, 32 * s + chunk + 1)
                    if on_pool(j, half):
                        wait(act, gated_pool, POOL_STEP * s + pool_gated(j) - 2)
                    dst = rl[j // 2 % 2] if on_pool(j, half) else ps[chunk % SRING]
                    c = chunk % CHUNKS
                    nc.scalar.activation(dst[:, :], ps[chunk % SRING][:, :], ACT.Relu,
                                         bias=b1s[:, c:c + 1]).then_inc(relu_done, 1)

            def embed(k, par):
                square_heads(k)
                roots(k)
                copy_ht(k, 0)
                copy_ht(k, 1)
                copy_t(k)

            def attend(k, par):
                square_again(k)
                root_again(k)
                round_hi(k, par, 0)
                round_hi(k, par, 1)
                spread_gates(k)
                copy_gates(k, par, 0)
                copy_gates(k, par, 1)

            def step(s, par, first=False, embeds=True, attends=True, feeds=True):
                for j in range(SLOTS):
                    if feeds:
                        relu_slot(s, j)
                    if not first and j == LAG - 1:
                        copy_y(s - 1, 1)
                    if embeds and j == 3:
                        square_heads(s + 2)
                    if embeds and j == 4:
                        roots(s + 2)
                    if attends and j == 4:
                        square_again(s + 1)
                    if attends and j == 5:
                        root_again(s + 1)
                    if embeds and j == 5:
                        copy_ht(s + 2, 0)
                    if embeds and j == 6:
                        copy_ht(s + 2, 1)
                    if attends and j == 7:
                        round_hi(s + 1, 1 - par, 0)
                    if attends and j == 8:
                        round_hi(s + 1, 1 - par, 1)
                    if not first and j == 8:
                        square_last(s - 1)
                    if feeds and j == SLOTS // 2 + LAG - 1:
                        copy_y(s, 0)
                    if not first and j == 10:
                        root_last(s - 1)
                    if embeds and j == 11:
                        copy_t(s + 2)
                    if attends and j == 12:
                        spread_gates(s + 1)
                    if attends and j == 13:
                        copy_gates(s + 1, 1 - par, 0)
                    if attends and j == 14:
                        copy_gates(s + 1, 1 - par, 1)

            pipeline(act, embed, attend, step)

        @block.vector
        def _(dve):
            dve.wait_ge(const_in, ALL_CONSTS)
            dve.wait_ge(w1_split, 1)
            nc.vector.tensor_tensor(w1l[:, :], w1f[:, :], w1h[:, :].bitcast(F32),
                                    ALU.subtract).then_inc(weights_ready, 1)
            nc.vector.tensor_tensor(blocks(posb), blocks(posb), over_blocks(tokb),
                                    ALU.add).then_inc(weights_ready, 1)
            nc.vector.tensor_scalar(kaug[0:C, :], eye[0:C, 0:C], kwv[:, 0:1], None,
                                    ALU.mult).then_inc(weights_ready, 1)
            nc.vector.tensor_scalar(vaug[0:C, :], eye[0:C, 0:C], kwv[:, 1:2], None,
                                    ALU.mult).then_inc(weights_ready, 1)
            dve.wait_ge(weights_ready, 4)

            def add_position(k, par):
                dve.wait_ge(embedded, k + 1)
                wait(dve, h2_ready, k - 1)
                nc.vector.tensor_tensor(h[par][:, :], pa[:, :], posb[:, :], ALU.add).then_inc(h_ready, 1)

            def head_sums(k, par):
                dve.wait_ge(h_ready, k + 1)
                nc.vector.tensor_reduce(hsum[:, :], heads(h[par]), AX_X, ALU.add).then_inc(sums_ready, 1)
                dve.wait_ge(sums_ready, k + 1)
                wait(dve, hcen_ready, k)
                nc.vector.tensor_reduce(sum1[:, :], hsum[:, :].rearrange("p (t g) -> p t g", g=HEADS),
                                        AX_X, ALU.add).then_inc(sum1_ready, 1)
                nc.vector.tensor_scalar(hmean[:, :], hsum[:, :], 1.0 / HD, None,
                                        ALU.mult).then_inc(hmean_ready, 1)
                dve.wait_ge(sum1_ready, k + 1)
                nc.vector.tensor_scalar(mean1[:, :], sum1[:, :], 1.0 / C, None,
                                        ALU.mult).then_inc(mean1_ready, 1)

            def center_heads(k, par):
                dve.wait_ge(hmean_ready, k + 1)
                nc.vector.tensor_tensor(heads(hc), heads(h[par]), per_head(hmean),
                                        ALU.subtract).then_inc(hc_ready, 1)
                dve.wait_ge(mean1_ready, k + 1)
                nc.vector.tensor_tensor(off[:, :].rearrange("p (t g) -> p t g", g=HEADS),
                                        hmean[:, :].rearrange("p (t g) -> p t g", g=HEADS),
                                        per_block(mean1, HEADS), ALU.subtract).then_inc(off_ready, 1)
                dve.wait_ge(off_ready, k + 1)
                nc.vector.tensor_tensor(off2[:, :], off[:, :], off[:, :], ALU.mult).then_inc(off2_ready, 1)

            def head_squares(k):
                dve.wait_ge(sq1_ready, k + 1)
                wait(dve, hstd_ready, k)
                nc.vector.tensor_reduce(hss[:, :], heads(sq1), AX_X, ALU.add).then_inc(hss_ready, 1)
                dve.wait_ge(hss_ready, k + 1)
                dve.wait_ge(off2_ready, k + 1)
                nc.vector.scalar_tensor_tensor(tss[:, :], off2[:, :], float(HD), hss[:, :], ALU.mult,
                                               ALU.add).then_inc(tss_ready, 1)
                dve.wait_ge(tss_ready, k + 1)
                nc.vector.tensor_reduce(ss1[:, :], tss[:, :].rearrange("p (t g) -> p t g", g=HEADS),
                                        AX_X, ALU.add).then_inc(ss1_ready, 1)

            def head_scales(k, par):
                dve.wait_ge(std1_ready, k + 1)
                nc.vector.reciprocal(rstd1[par][:, :], std1[:, :]).then_inc(rstd1_ready, 1)
                dve.wait_ge(rstd1_ready, k + 1)
                dve.wait_ge(hstd_ready, k + 1)

                def g3(buf):
                    return buf[:, :].rearrange("p (t g) -> p t g", g=HEADS)
                nc.vector.tensor_tensor(g3(den), g3(hstd), per_block(rstd1[par], HEADS),
                                        ALU.mult).then_inc(den_ready, 1)
                dve.wait_ge(den_ready, k + 1)
                nc.vector.tensor_scalar(den2[:, :], den[:, :], EPS, None, ALU.add).then_inc(den2_ready, 1)
                dve.wait_ge(den2_ready, k + 1)
                nc.vector.reciprocal(rden[:, :], den2[:, :]).then_inc(rden_ready, 1)
                dve.wait_ge(rden_ready, k + 1)
                nc.vector.tensor_tensor(g3(fac), g3(rden), per_block(rstd1[par], HEADS),
                                        ALU.mult).then_inc(fac_ready, 1)

            def normalise_heads(k):
                dve.wait_ge(fac_ready, k + 1)
                wait(dve, m_done, k)
                nc.vector.tensor_tensor(
                    naug[:, :, 0:C].rearrange("p t (g d) -> p t g d", d=HD),
                    hc[:, :].rearrange("p (t g d) -> p t g d", g=HEADS, d=HD),
                    fac[:, :].rearrange("p (t g) -> p t g", g=HEADS).unsqueeze(3)
                    .to_broadcast([P, T, HEADS, HD]), ALU.mult).then_inc(n_ready, 1)

            def copy_m(k):
                dve.wait_ge(m_done, k + 1)
                nc.vector.tensor_copy(maug[:, :], pa[0:C + 1, 0:C + 1]).then_inc(m_copied, 1)

            def attention_matrix(k):
                dve.wait_ge(kv_done, k + 1)
                nc.vector.tensor_tensor(am0[:, :], pa[0:C, 256:256 + C], mask_n[:, :],
                                        ALU.mult).then_inc(am0_ready, 1)
                dve.wait_ge(am0_ready, k + 1)
                wait(dve, attended, k)
                nc.vector.tensor_tensor(am[:, :], am0[:, :], eye[0:C, 0:C], ALU.add).then_inc(am_ready, 1)

            def scale_attention(k, par):
                dve.wait_ge(attended, k + 1)
                wait(dve, h2_ready, k)
                nc.vector.tensor_tensor(blocks(osc), blocks(pb), per_block(rstd1[par]),
                                        ALU.mult).then_inc(osc_ready, 1)

            def mean_again(k):
                dve.wait_ge(h2_ready, k + 1)
                nc.vector.tensor_reduce(sum2[:, :], blocks(h2), AX_X, ALU.add).then_inc(sum2_ready, 1)
                dve.wait_ge(sum2_ready, k + 1)
                wait(dve, cen2_ready, k)
                nc.vector.tensor_scalar(mean2[:, :], sum2[:, :], 1.0 / C, None,
                                        ALU.mult).then_inc(mean2_ready, 1)

            def squares_again(k):
                dve.wait_ge(sq2_ready, k + 1)
                wait(dve, std2_ready, k)
                nc.vector.tensor_reduce(ss2[:, :], blocks(sq2), AX_X, ALU.add).then_inc(ss2_ready, 1)

            def scale_again(k):
                dve.wait_ge(std2_ready, k + 1)
                wait(dve, xn_ready, k)
                nc.vector.reciprocal(rstd2[:, :], std2[:, :]).then_inc(rstd2_ready, 1)

            def split_lo(k, par, half):
                cols = slice(half * W, (half + 1) * W)
                dve.wait_ge(hi_ready, 2 * k + half + 1)
                nc.vector.tensor_tensor(xs[par][C:P, cols], pb[0:C, :], xs[par][0:C, cols].bitcast(F32),
                                        ALU.subtract).then_inc(lo_ready, 1)

            def top_two(k):
                dve.wait_ge(logits_done, k + 1)
                nc.vector.tensor_tensor(logit[:, :].rearrange("p (t e) -> p t e", e=NE),
                                        pb[:, 0:T * NE].rearrange("p (t e) -> p t e", e=NE),
                                        over_blocks(gbias, NE), ALU.add).then_inc(logit_ready, 1)
                dve.wait_ge(logit_ready, k + 1)
                settle(dve, "dve")
                for t in range(T):
                    last = nc.vector.max(top[:, t, :], logit[:, t * NE:(t + 1) * NE])
                last.then_inc(top_ready, 1)
                dve.wait_ge(top_ready, k + 1)
                wait(dve, egap_ready, k)
                nc.vector.tensor_tensor(gap[:, :], top[:, :, 1], top[:, :, 0],
                                        ALU.subtract).then_inc(gap_ready, 1)
                for t in range(T):
                    last = nc.vector.max_index(topi[:, t, :], top[:, t, :], logit[:, t * NE:(t + 1) * NE])
                last.then_inc(topi_ready, 1)
                dve.wait_ge(topi_ready, k + 1)
                nc.vector.tensor_copy(topf[:, :, :], topi[:, :, 0:2]).then_inc(topf_ready, 1)
                dve.wait_ge(topf_ready, k + 1)
                for hit, n in ((hit1, 0), (hit2, 1)):
                    last = nc.vector.tensor_tensor(
                        hit[:, :].rearrange("p (t e) -> p t e", e=NE), over_blocks(expert_no, NE),
                        topf[:, :, n:n + 1].to_broadcast([P, T, NE]), ALU.is_equal)
                last.then_inc(hits_ready, 1)

            def gate_values(k):
                dve.wait_ge(egap_ready, k + 1)
                nc.vector.tensor_scalar(gden[:, :], egap[:, :], 1.0, None, ALU.add).then_inc(gden_ready, 1)
                dve.wait_ge(gden_ready, k + 1)
                nc.vector.reciprocal(wt1[:, :], gden[:, :]).then_inc(wt1_ready, 1)
                dve.wait_ge(wt1_ready, k + 1)
                nc.vector.tensor_tensor(wt2[:, :], egap[:, :], wt1[:, :], ALU.mult).then_inc(wt2_ready, 1)
                dve.wait_ge(hits_ready, k + 1)
                dve.wait_ge(wt2_ready, k + 1)

                def e3(buf):
                    return buf[:, :].rearrange("p (t e) -> p t e", e=NE)
                nc.vector.tensor_tensor(e3(gat1), e3(hit1), per_block(wt1, NE), ALU.mult)
                nc.vector.tensor_tensor(e3(gat2), e3(hit2), per_block(wt2, NE),
                                        ALU.mult).then_inc(gats_ready, 1)
                dve.wait_ge(gats_ready, k + 1)
                wait(dve, spread_ready, k)
                nc.vector.tensor_tensor(gates[:, :], gat1[:, :], gat2[:, :], ALU.add).then_inc(gates_ready, 1)

            def gate_slot(s, par, j):
                for half in range(2):
                    if on_pool(j, half):
                        continue
                    chunk = 2 * j + half
                    dve.wait_ge(relu_done, 32 * s + chunk + 1)
                    if half == 0:
                        wait(dve, y_chunks, SLOTS * s + j - GRING // 2 + 1)
                        if j % (SLOTS // TILES) == 0:
                            dve.wait_ge(g_copied, 2 * s + j // (SLOTS // TILES) + 1)
                    cols = slice(j // (SLOTS // TILES) * W, (j // (SLOTS // TILES) + 1) * W)
                    nc.vector.tensor_tensor(hg[chunk % GRING][:, :], ps[chunk % SRING][:, :],
                                            gt[par][:, cols], ALU.mult).then_inc(gated_dve, 1)

            def add_ffn(k, par):
                dve.wait_ge(f_done, TILES * (k + 1))
                wait(dve, cen3_ready, k)
                nc.vector.tensor_tensor(ysum[:, :], pf[:, :], xn[par][:, :], ALU.add).then_inc(ysum_ready, 1)

            def mean_last(k):
                dve.wait_ge(ysum_ready, k + 1)
                nc.vector.tensor_reduce(sum3[:, :], blocks(ysum), AX_X, ALU.add).then_inc(sum3_ready, 1)
                dve.wait_ge(sum3_ready, k + 1)
                nc.vector.tensor_scalar(mean3[:, :], sum3[:, :], 1.0 / C, None,
                                        ALU.mult).then_inc(mean3_ready, 1)

            def squares_last(k):
                dve.wait_ge(sq3_ready, k + 1)
                wait(dve, std3_ready, k)
                nc.vector.tensor_reduce(ss3[:, :], blocks(sq3), AX_X, ALU.add).then_inc(ss3_ready, 1)

            def scale_last(k):
                dve.wait_ge(std3_ready, k + 1)
                nc.vector.reciprocal(rstd3[:, :], std3[:, :]).then_inc(rstd3_ready, 1)
                dve.wait_ge(rstd3_ready, k + 1)
                wait(dve, yg_ready, k)
                nc.vector.tensor_tensor(blocks(yn), blocks(cen3), per_block(rstd3),
                                        ALU.mult).then_inc(yn_ready, 1)

            def embed(k, par):
                add_position(k, par)
                head_sums(k, par)
                center_heads(k, par)
                head_squares(k)
                head_scales(k, par)
                normalise_heads(k)
                copy_m(k)
                attention_matrix(k)

            def attend(k, par):
                scale_attention(k, par)
                mean_again(k)
                squares_again(k)
                scale_again(k)
                split_lo(k, par, 0)
                split_lo(k, par, 1)
                top_two(k)
                gate_values(k)

            def step(s, par, first=False, embeds=True, attends=True, feeds=True):
                for j in range(SLOTS):
                    if feeds:
                        gate_slot(s, par, j)
                    if embeds and j == 0:
                        add_position(s + 2, par)
                    if embeds and j == 1:
                        head_sums(s + 2, par)
                    if attends and j == 1:
                        scale_attention(s + 1, 1 - par)
                    if embeds and j == 2:
                        center_heads(s + 2, par)
                    if attends and j == 3:
                        mean_again(s + 1)
                    if embeds and j == 4:
                        head_squares(s + 2)
                    if not first and j == 4:
                        add_ffn(s - 1, 1 - par)
                    if attends and j == 5:
                        squares_again(s + 1)
                    if embeds and j == 5:
                        head_scales(s + 2, par)
                    if attends and j == 6:
                        scale_again(s + 1)
                    if not first and j == 6:
                        mean_last(s - 1)
                    if embeds and j == 7:
                        normalise_heads(s + 2)
                    if attends and j == 8:
                        split_lo(s + 1, 1 - par, 0)
                    if attends and j == 9:
                        split_lo(s + 1, 1 - par, 1)
                    if not first and j == 9:
                        squares_last(s - 1)
                    if attends and j == 10:
                        top_two(s + 1)
                    if not first and j == 11:
                        scale_last(s - 1)
                    if embeds and j == 11:
                        copy_m(s + 2)
                    if attends and j == 12:
                        gate_values(s + 1)
                    if embeds and j == 14:
                        attention_matrix(s + 2)

            pipeline(dve, embed, attend, step)

        @block.tensor
        def _(pe):
            pe.wait_ge(const_in, ALL_CONSTS)
            pe.wait_ge(b2_in, 16)
            pe.wait_ge(weights_ready, 4)
            pe.wait_ge(ones_ready, 2)

            def embed_patches(k, par):
                pe.wait_ge(loaded, 16 * (k + 1))
                wait(pe, am0_ready, k)
                for t in range(T):
                    last = nc.tensor.matmul(pa[:, t * C:(t + 1) * C], xin[par][:, t * P:(t + 1) * P],
                                            wt[:, :], start=True, stop=True)
                last.then_inc(embedded, 1)

            def turn_tokens(k, half):
                pe.wait_ge(hcen_ready, k + 1)
                if half == 0:
                    pe.wait_ge(h_ready, k + 1)
                else:
                    pe.wait_ge(ht_copied, 2 * k + 1)
                settle(pe, "pe")
                for t in range(TT):
                    b = half * TT + t
                    last = nc.tensor.transpose(pa[0:C, t * P:(t + 1) * P], hcen[:, b * C:(b + 1) * C],
                                               eye[:, :])
                last.then_inc(ht_turned, 1)

            def gram(k):
                pe.wait_ge(n_ready, k + 1)
                pe.wait_ge(ht_copied, 2 * k + 2)
                for t in range(T):
                    last = nc.tensor.matmul(pa[0:C + 1, 0:C + 1], naug[:, t, :], naug[:, t, :],
                                            start=(t == 0), stop=(t == T - 1))
                last.then_inc(m_done, 1)

            def times_v(k):
                pe.wait_ge(m_copied, k + 1)
                nc.tensor.matmul(pa[0:C + 1, 128:128 + C], maug[:, :], vaug[:, :], start=True,
                                 stop=True).then_inc(t_done, 1)

            def times_k(k):
                pe.wait_ge(t_copied, k + 1)
                nc.tensor.matmul(pa[0:C, 256:256 + C], kaug[:, :], tm[:, :], start=True,
                                 stop=True).then_inc(kv_done, 1)

            def attention(k):
                pe.wait_ge(am_ready, k + 1)
                wait(pe, g_copied, 2 * k)
                for t in range(T):
                    last = nc.tensor.matmul(pb[:, t * C:(t + 1) * C], ht[:, t * P:(t + 1) * P], am[:, :],
                                            start=True, stop=True)
                last.then_inc(attended, 1)

            def turn_x(k, par, half):
                pe.wait_ge(xn_ready, k + 1)
                if half == 0:
                    pe.wait_ge(osc_ready, k + 1)
                else:
                    pe.wait_ge(lo_ready, 2 * k + 1)
                settle(pe, "pe")
                for t in range(TT):
                    b = half * TT + t
                    last = nc.tensor.transpose(pb[0:C, t * P:(t + 1) * P], xn[par][:, b * C:(b + 1) * C],
                                               eye[:, :])
                last.then_inc(x_turned, 1)

            def gate_logits(k, par):
                pe.wait_ge(lo_ready, 2 * k + 2)
                for t in range(T):
                    last = nc.tensor.matmul(pb[:, t * NE:(t + 1) * NE],
                                            xs[par][:, t * P:(t + 1) * P].bitcast(F32), gw2[:, :],
                                            start=True, stop=True)
                last.then_inc(logits_done, 1)

            def turn_gates(k, half):
                pe.wait_ge(spread_ready, k + 1)
                if half == 1:
                    pe.wait_ge(g_copied, 2 * k + 1)
                for t in range(TT):
                    b = half * TT + t
                    last = nc.tensor.transpose(pb[:, t * P:(t + 1) * P], spread[:, b * P:(b + 1) * P],
                                               eye[:, :])
                last.then_inc(g_turned, 1)

            def hidden(s, par, j):
                cols = slice(j // (SLOTS // TILES) * W, (j // (SLOTS // TILES) + 1) * W)
                for half in range(2):
                    chunk = 2 * j + half
                    c = chunk % CHUNKS
                    if half == 0:
                        wait(pe, gated_dve, DVE_STEP * s + (dve_gated(j - 2) if j >= 2 else
                                                            dve_gated(j + SLOTS - 2) - DVE_STEP))
                        wait(pe, relu_done, 32 * s + chunk - SRING + 2)
                    bank = ps[chunk % SRING]
                    nc.tensor.matmul(bank[:, :], w1h[:, c * P:(c + 1) * P], xs[par][:, cols],
                                     start=True, stop=False)
                    nc.tensor.matmul(bank[:, :], w1l[:, c * P:(c + 1) * P], xs[par][:, cols],
                                     start=False, stop=True).then_inc(s_done, 1)

            def combine(s, j):
                tile, first = j // (SLOTS // TILES), j % (SLOTS // TILES) == 0
                final = j % (SLOTS // TILES) == SLOTS // TILES - 1
                wait(pe, gated_dve, DVE_STEP * s + dve_gated(j))
                wait(pe, gated_pool, POOL_STEP * s + pool_gated(j))
                if first:
                    wait(pe, y_copied, TILES * s + tile)
                for half in range(2):
                    chunk = 2 * j + half
                    c = chunk % CHUNKS
                    last = nc.tensor.matmul(py[half * C:(half + 1) * C, :], w2s[:, c * C:(c + 1) * C],
                                            hg[chunk % GRING][:, :], start=first, stop=final,
                                            skip_group_check=True)
                last.then_inc(y_chunks, 1)

            def tokens_again(k, par, tile):
                pe.wait_ge(y_copied, TILES * k + tile + 1)
                wait(pe, ysum_ready, k)
                for t in range(TT):
                    b = tile * TT + t
                    nc.tensor.matmul(pf[:, b * C:(b + 1) * C], yt[tile][:, t * P:(t + 1) * P], eye2[:, :],
                                     start=True, stop=False)
                    last = nc.tensor.matmul(pf[:, b * C:(b + 1) * C], gt[par][:, b * P:(b + 1) * P],
                                            b2x[:, :], start=False, stop=True)
                last.then_inc(f_done, 1)

            def embed(k, par):
                embed_patches(k, par)
                turn_tokens(k, 0)
                turn_tokens(k, 1)
                gram(k)
                times_v(k)
                times_k(k)

            def attend(k, par):
                attention(k)
                turn_x(k, par, 0)
                turn_x(k, par, 1)
                gate_logits(k, par)
                turn_gates(k, 0)
                turn_gates(k, 1)

            def step(s, par, first=False, embeds=True, attends=True, feeds=True):
                for j in range(SLOTS):
                    if feeds:
                        hidden(s, par, j)
                    if j >= LAG and feeds:
                        combine(s, j - LAG)
                    if j < LAG and not first:
                        combine(s - 1, j + SLOTS - LAG)
                    if embeds and j == 0:
                        embed_patches(s + 2, par)
                    if attends and j == 1:
                        attention(s + 1)
                    if not first and j == 3:
                        tokens_again(s - 1, 1 - par, 1)
                    if embeds and j == 5:
                        turn_tokens(s + 2, 0)
                    if embeds and j == 6:
                        turn_tokens(s + 2, 1)
                    if attends and j == 7:
                        turn_x(s + 1, 1 - par, 0)
                    if attends and j == 8:
                        turn_x(s + 1, 1 - par, 1)
                    if attends and j == 9:
                        gate_logits(s + 1, 1 - par)
                    if embeds and j == 9:
                        gram(s + 2)
                    if feeds and j == 11:
                        tokens_again(s, par, 0)
                    if embeds and j == 11:
                        times_v(s + 2)
                    if embeds and j == 12:
                        times_k(s + 2)
                    if attends and j == 13:
                        turn_gates(s + 1, 0)
                    if attends and j == 14:
                        turn_gates(s + 1, 1)

            pipeline(pe, embed, attend, step)


def kernel(x, L0_tok_W, L0_tok_b, L0_tok_pos_embed, L0_attn_kln_weight, L0_attn_kln_bias,
           L0_attn_vln_weight, L0_attn_vln_bias, L0_ffn_gate_w, L0_ffn_gate_b, L0_ffn_w1, L0_ffn_b1,
           L0_ffn_w2, L0_ffn_b2, L0_ffn_gamma, L0_ffn_beta):
    import numpy as np
    import concourse.bacc as bacc
    from concourse.bass_utils import run_bass_kernel_spmd

    patches = np.asarray(x).reshape(B, 16, 8, 64, 8).transpose(0, 2, 4, 1, 3).reshape(B, C, P, T)
    w1 = np.asarray(L0_ffn_w1).reshape(NE, C, CHUNKS, UN).transpose(1, 2, 0, 3).reshape(C, CHUNKS * P)
    w2 = np.asarray(L0_ffn_w2).reshape(NE, CHUNKS, UN, C).transpose(0, 2, 1, 3).reshape(P, CHUNKS * C)
    b1 = np.asarray(L0_ffn_b1).reshape(NE, CHUNKS, UN).transpose(0, 2, 1).reshape(P, CHUNKS)
    head = np.arange(C) // HD
    numbers = np.zeros((P, NE + T), np.float32)
    numbers[:, :NE] = np.arange(NE)
    numbers[:, NE:] = np.e
    arrays = {
        "patches": patches.transpose(0, 1, 3, 2).reshape(B, C, N),
        "tok_w": np.asarray(L0_tok_W).T,
        "tok_b": L0_tok_b,
        "pos": np.asarray(L0_tok_pos_embed).reshape(P, T * C),
        "k_w": np.asarray(L0_attn_kln_weight).reshape(C),
        "k_b": np.asarray(L0_attn_kln_bias).reshape(C),
        "v_w": np.asarray(L0_attn_vln_weight).reshape(C),
        "v_b": np.asarray(L0_attn_vln_bias).reshape(C),
        "gate_w": L0_ffn_gate_w,
        "gate_b": L0_ffn_gate_b,
        "w1": w1,
        "b1": b1,
        "w2": w2,
        "b2": L0_ffn_b2,
        "gamma": L0_ffn_gamma,
        "beta": L0_ffn_beta,
        "ident": np.eye(P, dtype=np.float32),
        "head_mask": (head[:, None] == head[None, :]).astype(np.float32) / np.float32(N),
        "numbers": numbers,
    }
    nc = bacc.Bacc("TRN2", target_bir_lowering=False, num_devices=1)
    given, args = {}, []
    for name, a in arrays.items():
        a = np.ascontiguousarray(a)
        given[f"in_{name}"] = a
        args.append(nc.dram_tensor(f"in_{name}", a.shape, mybir.dt.from_np(a.dtype),
                                   kind="ExternalInput").ap())
    out = nc.dram_tensor("out", (B, P, T * C), F32, kind="ExternalOutput").ap()
    tower(nc, *args, out)
    r = run_bass_kernel_spmd(nc, [given], core_ids=[0])
    return r.results[0]["out"].reshape(B, N, C)
```

```python
from contextlib import ExitStack

import concourse.bass as bass
from concourse import mybir

F32 = mybir.dt.float32
F32R = mybir.dt.float32r
U32 = mybir.dt.uint32
ALU = mybir.AluOpType
ACT = mybir.ActivationFunctionType
AX_X = mybir.AxisListType.X

P = 128
B = 16
N = 1024
T = N // P
C = 64
HEADS = 8
HD = C // HEADS
GROUPS = T * HEADS
NE = 16
FH = 128
UN = P // NE
CHUNKS = FH // UN
W = 512
TILES = N // W
TT = W // P
STEP = CHUNKS * TILES
SRING = 4
GRING = 8
GROUP = 4
EPS = 1e-5


def on_pool(chunk):
    return chunk % 4 == 3


def dve_gated(chunk):
    return chunk // 4 * 3 + min(chunk % 4 + 1, 3)


def pool_gated(chunk):
    return (chunk + 1) // 4


DVE_STEP = dve_gated(STEP - 1)
POOL_STEP = pool_gated(STEP - 1)


def has(batch):
    return not isinstance(batch, int) or 0 <= batch < B


def tower(nc, patches, tok_w, tok_b, pos, k_w, k_b, v_w, v_b, gate_w, gate_b, w1, b1, w2, b2,
          gamma, beta, ident, head_mask, numbers, out):
    with ExitStack() as ctx:
        def sb(name, shape, dt=F32):
            return ctx.enter_context(nc.sbuf_tensor(name, shape, dt))

        def sem(name):
            return ctx.enter_context(nc.semaphore(name))

        eye = sb("eye", [P, P])
        eye2 = sb("eye2", [P, C])
        mask_n = sb("mask_n", [C, C])
        expert_no = sb("expert_no", [P, NE])
        euler = sb("euler", [P, T])
        wt = sb("wt", [C, C])
        posb = sb("posb", [P, T * C])
        tokb = sb("tokb", [P, C])
        kaug = sb("kaug", [C + 1, C])
        vaug = sb("vaug", [C + 1, C])
        kwv = sb("kwv", [C, 2])
        gw2 = sb("gw2", [P, NE])
        gwr = sb("gwr", [P, 2 * NE], F32R)
        gbias = sb("gbias", [P, NE])
        w1f = sb("w1f", [P, CHUNKS * P])
        w1h = sb("w1h", [P, CHUNKS * P], F32R)
        w1l = sb("w1l", [P, CHUNKS * P], F32R)
        w2s = sb("w2s", [P, CHUNKS * C])
        b1s = sb("b1s", [P, CHUNKS])
        b2x = sb("b2x", [P, C])
        gam = sb("gam", [P, C])
        bet = sb("bet", [P, C])
        epsc = sb("epsc", [P, 1])
        xin = [sb(f"xin{i}", [C, N]) for i in range(2)]
        h = [sb(f"h{i}", [P, T * C]) for i in range(2)]
        rstd1 = [sb(f"rstd1{i}", [P, T]) for i in range(2)]
        hsum = sb("hsum", [P, GROUPS])
        hmean = sb("hmean", [P, GROUPS])
        sum1 = sb("sum1", [P, T])
        mean1 = sb("mean1", [P, T])
        off = sb("off", [P, GROUPS])
        off2 = sb("off2", [P, GROUPS])
        hc = sb("hc", [P, T * C])
        sq1 = sb("sq1", [P, T * C])
        hss = sb("hss", [P, GROUPS])
        tss = sb("tss", [P, GROUPS])
        ss1 = sb("ss1", [P, T])
        std1 = sb("std1", [P, T])
        hstd = sb("hstd", [P, GROUPS])
        den = sb("den", [P, GROUPS])
        den2 = sb("den2", [P, GROUPS])
        rden = sb("rden", [P, GROUPS])
        fac = sb("fac", [P, GROUPS])
        naug = sb("naug", [P, T, C + 1])
        hcen = sb("hcen", [P, T * C])
        ht = sb("ht", [C, N])
        maug = sb("maug", [C + 1, C + 1])
        tm = sb("tm", [C + 1, C])
        am0 = sb("am0", [C, C])
        am = sb("am", [C, C])
        osc = sb("osc", [P, T * C])
        h2 = sb("h2", [P, T * C])
        halves = sb("halves", [P, T, 6])
        stats2 = sb("stats2", [P, T, 2])
        cen2 = sb("cen2", [P, T * C])
        std2 = sb("std2", [P, T])
        rstd2 = sb("rstd2", [P, T])
        xn = sb("xn", [P, T * C])
        xk = [sb(f"xk{i}", [P, T * C]) for i in range(2)]
        hb = [sb(f"hb{i}", [P, T * C]) for i in range(2)]
        xs = [sb(f"xs{i}", [P, N], F32R) for i in range(2)]
        part = sb("part", [P, T * NE])
        logit = sb("logit", [P, T * NE])
        top = sb("top", [P, T, 8])
        topi = sb("topi", [P, T, 8], U32)
        topf = sb("topf", [P, T, 2])
        gap = sb("gap", [P, T])
        egap = sb("egap", [P, T])
        gden = sb("gden", [P, T])
        wt1 = sb("wt1", [P, T])
        wt2 = sb("wt2", [P, T])
        hit1 = sb("hit1", [P, T * NE])
        hit2 = sb("hit2", [P, T * NE])
        gat1 = sb("gat1", [P, T * NE])
        gat2 = sb("gat2", [P, T * NE])
        gates = sb("gates", [P, T * NE])
        spread = sb("spread", [P, N])
        gt = [sb(f"gt{i}", [P, N]) for i in range(2)]
        rl = [sb(f"rl{i}", [P, W]) for i in range(2)]
        hg = [sb(f"hg{i}", [P, W]) for i in range(GRING)]
        yt = [sb(f"yt{i}", [P, W]) for i in range(TILES)]
        ysum = sb("ysum", [P, T * C])
        sum3 = sb("sum3", [P, T])
        mean3 = sb("mean3", [P, T])
        cen3 = sb("cen3", [P, T * C])
        sq3 = sb("sq3", [P, T * C])
        ss3 = sb("ss3", [P, T])
        std3 = sb("std3", [P, T])
        rstd3 = sb("rstd3", [P, T])
        yn = sb("yn", [P, T * C])
        yg = sb("yg", [P, T * C])
        res = sb("res", [P, T * C])

        ps = [ctx.enter_context(nc.psum_tensor(f"ps{i}", [P, W], F32)) for i in range(SRING)]
        py = ctx.enter_context(nc.psum_tensor("py", [P, W], F32))
        pf = ctx.enter_context(nc.psum_tensor("pf", [P, W], F32))
        pa = ctx.enter_context(nc.psum_tensor("pa", [P, W], F32))
        pb = ctx.enter_context(nc.psum_tensor("pb", [P, W], F32))

        const_in = sem("const_in")
        b2_in = sem("b2_in")
        w1_split, weights_ready, ones_ready, zero_ready = (
            sem(x) for x in ("w1_split", "weights_ready", "ones_ready", "zero_ready"))
        loaded, stored = sem("loaded"), sem("stored")
        embedded, h_ready, sums_ready, hmean_ready, mean1_ready, off_ready, off2_ready = (
            sem(x) for x in ("embedded", "h_ready", "sums_ready", "hmean_ready", "mean1_ready",
                             "off_ready", "off2_ready"))
        sum1_ready, hc_ready, sq1_ready, hss_ready, tss_ready, ss1_ready, std1_ready, hstd_ready = (
            sem(x) for x in ("sum1_ready", "hc_ready", "sq1_ready", "hss_ready", "tss_ready",
                             "ss1_ready", "std1_ready", "hstd_ready"))
        rstd1_ready, den_ready, den2_ready, rden_ready, fac_ready, n_ready, hcen_ready = (
            sem(x) for x in ("rstd1_ready", "den_ready", "den2_ready", "rden_ready", "fac_ready",
                             "n_ready", "hcen_ready"))
        ht_turned, ht_copied = sem("ht_turned"), sem("ht_copied")
        m_done, m_copied, t_done, t_copied, kv_done, am0_ready, am_ready = (
            sem(x) for x in ("m_done", "m_copied", "t_done", "t_copied", "kv_done", "am0_ready",
                             "am_ready"))
        attended, osc_ready, h2_ready, halves_ready, stats_ready, cen2_ready = (
            sem(x) for x in ("attended", "osc_ready", "h2_ready", "halves_ready", "stats_ready",
                             "cen2_ready"))
        std2_ready, rstd2_ready, xn_ready, xk_ready, hb_ready = (
            sem(x) for x in ("std2_ready", "rstd2_ready", "xn_ready", "xk_ready", "hb_ready"))
        x_turned, hi_ready, lo_ready = sem("x_turned"), sem("hi_ready"), sem("lo_ready")
        logits_done, logit_ready, top_ready, topi_ready, topf_ready, gap_ready, egap_ready = (
            sem(x) for x in ("logits_done", "logit_ready", "top_ready", "topi_ready", "topf_ready",
                             "gap_ready", "egap_ready"))
        gden_ready, wt1_ready, wt2_ready, hits_ready, gats_ready, gates_ready = (
            sem(x) for x in ("gden_ready", "wt1_ready", "wt2_ready", "hits_ready", "gats_ready",
                             "gates_ready"))
        spread_ready, part_ready = sem("spread_ready"), sem("part_ready")
        g_turned, g_copied = sem("g_turned"), sem("g_copied")
        s_done, relu_done = sem("s_done"), sem("relu_done")
        gated_dve, gated_pool = sem("gated_dve"), sem("gated_pool")
        y_pairs, y_copied, f_done = sem("y_pairs"), sem("y_copied"), sem("f_done")
        passed = {e: sem(f"passed_{e}") for e in ("pe", "dve", "sp")}
        ysum_ready, sum3_ready, mean3_ready, cen3_ready, sq3_ready, ss3_ready, std3_ready = (
            sem(x) for x in ("ysum_ready", "sum3_ready", "mean3_ready", "cen3_ready", "sq3_ready",
                             "ss3_ready", "std3_ready"))
        rstd3_ready, yn_ready, yg_ready, res_ready = (
            sem(x) for x in ("rstd3_ready", "yn_ready", "yg_ready", "res_ready"))

        def wait(eng, s, value):
            if not isinstance(value, int) or value > 0:
                eng.wait_ge(s, value)

        def tile_of(q):
            return slice(q // CHUNKS * W, (q // CHUNKS + 1) * W)

        def settle(eng, name):
            eng.sem_inc(passed[name], 1)

        def blocks(buf):
            return buf[:, :].rearrange("p (t c) -> p t c", t=T)

        def heads(buf):
            return buf[:, :].rearrange("p (g d) -> p g d", d=HD)

        def per_block(small, n=C):
            return small[:, :].unsqueeze(2).to_broadcast([P, T, n])

        def per_head(small):
            return small[:, :].unsqueeze(2).to_broadcast([P, GROUPS, HD])

        def over_blocks(row, n=C):
            return row[:, :].unsqueeze(1).to_broadcast([P, T, n])

        CONSTS = [
            (eye[:, :], ident[:, :]), (eye2[0:C, :], ident[0:C, 0:C]), (eye2[C:P, :], ident[0:C, 0:C]),
            (mask_n[:, :], head_mask[:, :]), (expert_no[:, :], numbers[:, 0:NE]),
            (euler[:, :], numbers[:, NE:NE + T]), (wt[:, :], tok_w[:, :]), (posb[:, :], pos[:, :]),
            (tokb[:, :], tok_b.unsqueeze(0).to_broadcast([P, C])),
            (kwv[:, 0:1], k_w.unsqueeze(1)), (kwv[:, 1:2], v_w.unsqueeze(1)),
            (kaug[C:C + 1, :], k_b.unsqueeze(0)), (vaug[C:C + 1, :], v_b.unsqueeze(0)),
            (gw2[0:C, :], gate_w[:, :]), (gw2[C:P, :], gate_w[:, :]),
            (gbias[:, :], gate_b.unsqueeze(0).to_broadcast([P, NE])),
            (w1f[0:C, :], w1[:, :]), (w1f[C:P, :], w1[:, :]), (w2s[:, :], w2[:, :]),
            (b1s[:, :], b1[:, :]),
            (gam[:, :], gamma.unsqueeze(0).to_broadcast([P, C])),
            (bet[:, :], beta.unsqueeze(0).to_broadcast([P, C])),
        ]
        ALL_CONSTS = 16 * len(CONSTS)

        def pipeline(eng, step):
            for s in range(-3, 2):
                step(s, s % 2)
            with eng.Fori(0, (B - 6) // 2) as i:
                step(2 * i + 2, 0)
                step(2 * i + 3, 1)
            for s in range(B - 4, B + 1):
                step(s, s % 2)

        block = ctx.enter_context(nc.Block())

        @block.sync
        def _(sp):
            for dst, src in CONSTS[:len(CONSTS) // 2]:
                sp.dma_start(dst, src).then_inc(const_in, 16)

            def load(k, par):
                wait(sp, loaded, 16 * k)
                settle(sp, "sp")
                wait(sp, embedded, k - 1)
                settle(sp, "sp")
                sp.dma_start(xin[par][:, :], patches[k, :, :] if isinstance(k, int)
                             else patches[bass.ds(k, 1), :, :].rearrange("a c n -> (a c) n")).then_inc(loaded, 16)

            def store(k):
                wait(sp, stored, 16 * k)
                settle(sp, "sp")
                sp.wait_ge(res_ready, k + 1)
                settle(sp, "sp")
                dst = out[k, :, :] if isinstance(k, int) else \
                    out[bass.ds(k, 1), :, :].rearrange("a p n -> (a p) n")
                sp.dma_start(dst, res[:, :]).then_inc(stored, 16)

            def step(s, par):
                if has(s + 3):
                    load(s + 3, 1 - par)
                if has(s - 1):
                    store(s - 1)

            pipeline(sp, step)
            sp.wait_ge(stored, 16 * B)

        @block.gpsimd
        def _(pool):
            nc.gpsimd.memset(b2x[:, :], 0.0).then_inc(zero_ready, 1)
            nc.gpsimd.memset(naug[:, :, C:C + 1], 1.0).then_inc(ones_ready, 1)
            nc.gpsimd.memset(epsc[:, :], EPS).then_inc(ones_ready, 1)
            pool.wait_ge(zero_ready, 1)
            pool.dma_start(b2x[0:P:UN, :], b2[:, :]).then_inc(b2_in, 16)
            pool.wait_ge(const_in, ALL_CONSTS)

            def center_tokens(k, par):
                pool.wait_ge(mean1_ready, k + 1)
                wait(pool, ht_turned, 2 * k)
                nc.gpsimd.tensor_tensor(blocks(hcen), blocks(h[par]), per_block(mean1),
                                        ALU.subtract).then_inc(hcen_ready, 1)

            def add_attention(k, par):
                pool.wait_ge(osc_ready, k + 1)
                wait(pool, hb_ready, k)
                nc.gpsimd.tensor_tensor(h2[:, :], osc[:, :], h[par][:, :], ALU.add).then_inc(h2_ready, 1)

            def center_again(k):
                pool.wait_ge(stats_ready, k + 1)
                pool.wait_ge(h2_ready, k + 1)
                wait(pool, xn_ready, k)
                nc.gpsimd.tensor_tensor(blocks(cen2), blocks(h2), stats2[:, :, 0:1].to_broadcast([P, T, C]),
                                        ALU.subtract).then_inc(cen2_ready, 1)

            def scale_again(k):
                pool.wait_ge(rstd2_ready, k + 1)
                pool.wait_ge(cen2_ready, k + 1)
                wait(pool, xk_ready, k)
                nc.gpsimd.tensor_tensor(blocks(xn), blocks(cen2), per_block(rstd2),
                                        ALU.mult).then_inc(xn_ready, 1)

            def exp_gap(k):
                pool.wait_ge(gap_ready, k + 1)
                wait(pool, wt2_ready, k)
                nc.gpsimd.tensor_tensor(egap[:, :], euler[:, :], gap[:, :], ALU.pow).then_inc(egap_ready, 1)

            def add_beta(k, par):
                pool.wait_ge(h2_ready, k + 1)
                wait(pool, res_ready, k - 1)
                nc.gpsimd.tensor_tensor(blocks(hb[par]), blocks(h2), over_blocks(bet),
                                        ALU.add).then_inc(hb_ready, 1)

            def center_last(k):
                pool.wait_ge(mean3_ready, k + 1)
                wait(pool, yn_ready, k)
                nc.gpsimd.tensor_tensor(blocks(cen3), blocks(ysum), per_block(mean3),
                                        ALU.subtract).then_inc(cen3_ready, 1)

            def times_gamma(k):
                pool.wait_ge(yn_ready, k + 1)
                nc.gpsimd.tensor_tensor(blocks(yg), blocks(yn), over_blocks(gam),
                                        ALU.mult).then_inc(yg_ready, 1)

            def add_residual(k, par):
                pool.wait_ge(yg_ready, k + 1)
                wait(pool, stored, 16 * k)
                nc.gpsimd.tensor_tensor(res[:, :], yg[:, :], hb[par][:, :], ALU.add).then_inc(res_ready, 1)

            def gate_chunk(s, par, q):
                pool.wait_ge(relu_done, STEP * s + q + 1)
                wait(pool, y_pairs, STEP // 2 * s + (q - GRING) // 2 + 1)
                if q % CHUNKS < 4:
                    pool.wait_ge(g_copied, 2 * s + q // CHUNKS + 1)
                nc.gpsimd.tensor_tensor(hg[q % GRING][:, :], rl[q // 4 % 2][:, :], gt[par][:, tile_of(q)],
                                        ALU.mult).then_inc(gated_pool, 1)

            def step(s, par):
                for q in range(STEP):
                    if has(s) and on_pool(q):
                        gate_chunk(s, par, q)
                    if q == 0 and has(s + 1):
                        center_again(s + 1)
                    if q == 2 and has(s + 1):
                        scale_again(s + 1)
                    if q == 12 and has(s - 1):
                        center_last(s - 1)
                    if q == 14 and has(s + 1):
                        exp_gap(s + 1)
                    if q == 20 and has(s - 1):
                        times_gamma(s - 1)
                    if q == 22 and has(s - 1):
                        add_residual(s - 1, 1 - par)
                    if q == 24 and has(s + 1):
                        add_beta(s + 1, 1 - par)
                    if q == 27 and has(s + 3):
                        center_tokens(s + 3, 1 - par)
                    if q == 28 and has(s + 2):
                        add_attention(s + 2, par)

            pipeline(pool, step)

        @block.scalar
        def _(act):
            for dst, src in CONSTS[len(CONSTS) // 2:]:
                act.dma_start(dst, src).then_inc(const_in, 16)
            act.wait_ge(const_in, ALL_CONSTS)
            act.wait_ge(ones_ready, 2)
            nc.scalar.activation(w1h[:, :], w1f[:, :], ACT.Copy).then_inc(w1_split, 1)
            nc.scalar.activation(gwr[:, 0:NE], gw2[:, :], ACT.Copy).then_inc(w1_split, 1)

            def square_heads(k):
                act.wait_ge(hc_ready, k + 1)
                wait(act, hss_ready, k)
                nc.scalar.activation(sq1[:, :], hc[:, :], ACT.Square).then_inc(sq1_ready, 1)

            def roots(k):
                act.wait_ge(ss1_ready, k + 1)
                nc.scalar.activation(std1[:, :], ss1[:, :], ACT.Sqrt, bias=epsc[:, 0:1],
                                     scale=1.0 / C).then_inc(std1_ready, 1)
                nc.scalar.activation(hstd[:, :], hss[:, :], ACT.Sqrt,
                                     scale=1.0 / (HD - 1)).then_inc(hstd_ready, 1)

            def copy_ht(k, half):
                act.wait_ge(ht_turned, 2 * k + half + 1)
                wait(act, attended, k)
                nc.scalar.activation(ht[:, half * W:(half + 1) * W], (pa, pf)[half][0:C, :],
                                     ACT.Copy).then_inc(ht_copied, 1)

            def copy_t(k):
                act.wait_ge(t_done, k + 1)
                nc.scalar.activation(tm[:, :], pa[0:C + 1, 128:128 + C], ACT.Copy).then_inc(t_copied, 1)

            def root_again(k):
                act.wait_ge(stats_ready, k + 1)
                wait(act, rstd2_ready, k)
                nc.scalar.activation(std2[:, :], stats2[:, :, 1], ACT.Sqrt,
                                     bias=epsc[:, 0:1]).then_inc(std2_ready, 1)

            def keep_xn(k, par):
                act.wait_ge(xn_ready, k + 1)
                wait(act, ysum_ready, k - 1)
                nc.scalar.activation(xk[par][:, :], xn[:, :], ACT.Copy).then_inc(xk_ready, 1)

            def round_hi(k, par, half):
                act.wait_ge(x_turned, 2 * k + half + 1)
                nc.scalar.activation(xs[par][0:C, half * W:(half + 1) * W], (pb, pa)[half][0:C, :],
                                     ACT.Copy).then_inc(hi_ready, 1)

            def spread_gates(k):
                act.wait_ge(gates_ready, k + 1)
                wait(act, g_turned, 2 * k)
                nc.scalar.activation(spread[:, :].rearrange("p (g u) -> p g u", u=UN),
                                     gates[:, :].unsqueeze(2).to_broadcast([P, T * NE, UN]),
                                     ACT.Copy).then_inc(spread_ready, 1)

            def copy_gates(k, par, half):
                act.wait_ge(g_turned, 2 * k + half + 1)
                wait(act, f_done, k - 1)
                nc.scalar.activation(gt[par][:, half * W:(half + 1) * W], (pb, pf)[half][:, :],
                                     ACT.Copy).then_inc(g_copied, 1)

            def copy_y(k, tile):
                act.wait_ge(y_pairs, STEP // 2 * k + CHUNKS // 2 * (tile + 1))
                wait(act, f_done, k)
                nc.scalar.activation(yt[tile][:, :], py[:, :], ACT.Copy).then_inc(y_copied, 1)

            def square_last(k):
                act.wait_ge(cen3_ready, k + 1)
                wait(act, ss3_ready, k)
                nc.scalar.activation(sq3[:, :], cen3[:, :], ACT.Square).then_inc(sq3_ready, 1)

            def root_last(k):
                act.wait_ge(ss3_ready, k + 1)
                nc.scalar.activation(std3[:, :], ss3[:, :], ACT.Sqrt, bias=epsc[:, 0:1],
                                     scale=1.0 / C).then_inc(std3_ready, 1)

            def relu(s, q):
                act.wait_ge(s_done, STEP * s + q + 1)
                if on_pool(q):
                    wait(act, gated_pool, POOL_STEP * s + pool_gated(q) - 2)
                dst = rl[q // 4 % 2] if on_pool(q) else ps[q % SRING]
                c = q % CHUNKS
                nc.scalar.activation(dst[:, :], ps[q % SRING][:, :], ACT.Relu,
                                     bias=b1s[:, c:c + 1]).then_inc(relu_done, 1)

            def step(s, par):
                for q in range(STEP):
                    if has(s):
                        relu(s, q)
                    if q == 1 and has(s + 1):
                        root_again(s + 1)
                    if q == 2 and has(s + 2):
                        roots(s + 2)
                    if q == GROUP - 1 and has(s - 1):
                        copy_y(s - 1, 1)
                    if q == 7 and has(s + 1):
                        round_hi(s + 1, 1 - par, 0)
                    if q == 8 and has(s + 1):
                        round_hi(s + 1, 1 - par, 1)
                    if q == 12 and has(s + 2):
                        copy_ht(s + 2, 0)
                    if q == 13 and has(s + 2):
                        copy_ht(s + 2, 1)
                    if q == 14 and has(s - 1):
                        square_last(s - 1)
                    if q == 17 and has(s - 1):
                        root_last(s - 1)
                    if q == CHUNKS + GROUP - 1 and has(s):
                        copy_y(s, 0)
                    if q == 21 and has(s + 2):
                        copy_t(s + 2)
                    if q == 22 and has(s + 1):
                        keep_xn(s + 1, 1 - par)
                    if q == 24 and has(s + 1):
                        spread_gates(s + 1)
                    if q == 27 and has(s + 1):
                        copy_gates(s + 1, 1 - par, 0)
                    if q == 28 and has(s + 1):
                        copy_gates(s + 1, 1 - par, 1)
                    if q == 29 and has(s + 3):
                        square_heads(s + 3)

            pipeline(act, step)

        @block.vector
        def _(dve):
            dve.wait_ge(const_in, ALL_CONSTS)
            dve.wait_ge(w1_split, 2)
            nc.vector.tensor_tensor(gwr[:, NE:2 * NE], gw2[:, :], gwr[:, 0:NE].bitcast(F32),
                                    ALU.subtract).then_inc(weights_ready, 1)
            nc.vector.tensor_tensor(w1l[:, :], w1f[:, :], w1h[:, :].bitcast(F32),
                                    ALU.subtract).then_inc(weights_ready, 1)
            nc.vector.tensor_tensor(blocks(posb), blocks(posb), over_blocks(tokb),
                                    ALU.add).then_inc(weights_ready, 1)
            nc.vector.tensor_scalar(kaug[0:C, :], eye[0:C, 0:C], kwv[:, 0:1], None,
                                    ALU.mult).then_inc(weights_ready, 1)
            nc.vector.tensor_scalar(vaug[0:C, :], eye[0:C, 0:C], kwv[:, 1:2], None,
                                    ALU.mult).then_inc(weights_ready, 1)
            dve.wait_ge(weights_ready, 5)

            def add_position(k, par):
                dve.wait_ge(embedded, k + 1)
                wait(dve, h2_ready, k - 1)
                nc.vector.tensor_tensor(h[par][:, :], pf[:, :], posb[:, :], ALU.add).then_inc(h_ready, 1)

            def head_sums(k, par):
                dve.wait_ge(h_ready, k + 1)
                nc.vector.tensor_reduce(hsum[:, :], heads(h[par]), AX_X, ALU.add).then_inc(sums_ready, 1)

            def token_sums(k):
                dve.wait_ge(sums_ready, k + 1)
                wait(dve, hcen_ready, k)
                nc.vector.tensor_reduce(sum1[:, :], hsum[:, :].rearrange("p (t g) -> p t g", g=HEADS),
                                        AX_X, ALU.add).then_inc(sum1_ready, 1)
                nc.vector.tensor_scalar(hmean[:, :], hsum[:, :], 1.0 / HD, None,
                                        ALU.mult).then_inc(hmean_ready, 1)

            def token_mean(k):
                dve.wait_ge(sum1_ready, k + 1)
                nc.vector.tensor_scalar(mean1[:, :], sum1[:, :], 1.0 / C, None,
                                        ALU.mult).then_inc(mean1_ready, 1)

            def center_heads(k, par):
                dve.wait_ge(hmean_ready, k + 1)
                nc.vector.tensor_tensor(heads(hc), heads(h[par]), per_head(hmean),
                                        ALU.subtract).then_inc(hc_ready, 1)

            def head_offsets(k):
                dve.wait_ge(mean1_ready, k + 1)
                nc.vector.tensor_tensor(off[:, :].rearrange("p (t g) -> p t g", g=HEADS),
                                        hmean[:, :].rearrange("p (t g) -> p t g", g=HEADS),
                                        per_block(mean1, HEADS), ALU.subtract).then_inc(off_ready, 1)

            def square_offsets(k):
                dve.wait_ge(off_ready, k + 1)
                nc.vector.tensor_tensor(off2[:, :], off[:, :], off[:, :], ALU.mult).then_inc(off2_ready, 1)

            def head_squares(k):
                dve.wait_ge(sq1_ready, k + 1)
                wait(dve, hstd_ready, k)
                nc.vector.tensor_reduce(hss[:, :], heads(sq1), AX_X, ALU.add).then_inc(hss_ready, 1)

            def token_parts(k):
                dve.wait_ge(hss_ready, k + 1)
                dve.wait_ge(off2_ready, k + 1)
                nc.vector.scalar_tensor_tensor(tss[:, :], off2[:, :], float(HD), hss[:, :], ALU.mult,
                                               ALU.add).then_inc(tss_ready, 1)

            def token_squares(k):
                dve.wait_ge(tss_ready, k + 1)
                nc.vector.tensor_reduce(ss1[:, :], tss[:, :].rearrange("p (t g) -> p t g", g=HEADS),
                                        AX_X, ALU.add).then_inc(ss1_ready, 1)

            def groups(buf):
                return buf[:, :].rearrange("p (t g) -> p t g", g=HEADS)

            def token_scale(k, par):
                dve.wait_ge(std1_ready, k + 1)
                nc.vector.reciprocal(rstd1[par][:, :], std1[:, :]).then_inc(rstd1_ready, 1)

            def scale_head_std(k, par):
                dve.wait_ge(rstd1_ready, k + 1)
                dve.wait_ge(hstd_ready, k + 1)
                nc.vector.tensor_tensor(groups(den), groups(hstd), per_block(rstd1[par], HEADS),
                                        ALU.mult).then_inc(den_ready, 1)

            def add_eps(k):
                dve.wait_ge(den_ready, k + 1)
                nc.vector.tensor_scalar(den2[:, :], den[:, :], EPS, None, ALU.add).then_inc(den2_ready, 1)

            def invert_heads(k):
                dve.wait_ge(den2_ready, k + 1)
                nc.vector.reciprocal(rden[:, :], den2[:, :]).then_inc(rden_ready, 1)

            def head_factors(k, par):
                dve.wait_ge(rden_ready, k + 1)
                nc.vector.tensor_tensor(groups(fac), groups(rden), per_block(rstd1[par], HEADS),
                                        ALU.mult).then_inc(fac_ready, 1)

            def normalise_heads(k):
                dve.wait_ge(fac_ready, k + 1)
                wait(dve, m_done, k)
                nc.vector.tensor_tensor(
                    naug[:, :, 0:C].rearrange("p t (g d) -> p t g d", d=HD),
                    hc[:, :].rearrange("p (t g d) -> p t g d", g=HEADS, d=HD),
                    fac[:, :].rearrange("p (t g) -> p t g", g=HEADS).unsqueeze(3)
                    .to_broadcast([P, T, HEADS, HD]), ALU.mult).then_inc(n_ready, 1)

            def copy_m(k):
                dve.wait_ge(m_done, k + 1)
                nc.vector.tensor_copy(maug[:, :], pa[0:C + 1, 0:C + 1]).then_inc(m_copied, 1)

            def attention_matrix(k):
                dve.wait_ge(kv_done, k + 1)
                nc.vector.tensor_tensor(am0[:, :], pa[0:C, 256:256 + C], mask_n[:, :],
                                        ALU.mult).then_inc(am0_ready, 1)

            def add_identity(k):
                dve.wait_ge(am0_ready, k + 1)
                wait(dve, attended, k)
                nc.vector.tensor_tensor(am[:, :], am0[:, :], eye[0:C, 0:C], ALU.add).then_inc(am_ready, 1)

            def scale_attention(k, par):
                dve.wait_ge(attended, k + 1)
                wait(dve, h2_ready, k)
                nc.vector.tensor_tensor(blocks(osc), blocks(pa), per_block(rstd1[par]),
                                        ALU.mult).then_inc(osc_ready, 1)

            def statistics(k):
                dve.wait_ge(h2_ready, k + 1)
                settle(dve, "dve")
                for t in range(T):
                    last = nc.vector.bn_stats(halves[:, t, :], h2[:, t * C:(t + 1) * C])
                last.then_inc(halves_ready, 1)

            def aggregate(k):
                dve.wait_ge(halves_ready, k + 1)
                wait(dve, cen2_ready, k)
                wait(dve, std2_ready, k)
                settle(dve, "dve")
                for t in range(T):
                    last = nc.vector.bn_aggr(stats2[:, t, :], halves[:, t, :])
                last.then_inc(stats_ready, 1)

            def scale_again(k):
                dve.wait_ge(std2_ready, k + 1)
                wait(dve, xn_ready, k)
                nc.vector.reciprocal(rstd2[:, :], std2[:, :]).then_inc(rstd2_ready, 1)

            def split_lo(k, par, half):
                cols = slice(half * W, (half + 1) * W)
                dve.wait_ge(hi_ready, 2 * k + half + 1)
                nc.vector.tensor_tensor(xs[par][C:P, cols], (pb, pa)[half][0:C, :], xs[par][0:C, cols].bitcast(F32),
                                        ALU.subtract).then_inc(lo_ready, 1)

            def experts(buf):
                return buf[:, :].rearrange("p (t e) -> p t e", e=NE)

            def add_gate_bias(k):
                dve.wait_ge(logits_done, k + 1)
                both = pb[:, 0:2 * T * NE].rearrange("p (t n e) -> p t n e", n=2, e=NE)
                nc.vector.tensor_tensor(experts(part), both[:, :, 1, :], over_blocks(gbias, NE),
                                        ALU.add).then_inc(part_ready, 1)

            def add_hi_part(k):
                dve.wait_ge(part_ready, k + 1)
                both = pb[:, 0:2 * T * NE].rearrange("p (t n e) -> p t n e", n=2, e=NE)
                nc.vector.tensor_tensor(experts(logit), both[:, :, 0, :], experts(part),
                                        ALU.add).then_inc(logit_ready, 1)

            def top_values(k):
                dve.wait_ge(logit_ready, k + 1)
                settle(dve, "dve")
                for t in range(T):
                    last = nc.vector.max(top[:, t, :], logit[:, t * NE:(t + 1) * NE])
                last.then_inc(top_ready, 1)

            def top_gap(k):
                dve.wait_ge(top_ready, k + 1)
                wait(dve, egap_ready, k)
                nc.vector.tensor_tensor(gap[:, :], top[:, :, 1], top[:, :, 0],
                                        ALU.subtract).then_inc(gap_ready, 1)

            def top_places(k):
                for t in range(T):
                    last = nc.vector.max_index(topi[:, t, :], top[:, t, :], logit[:, t * NE:(t + 1) * NE])
                last.then_inc(topi_ready, 1)

            def places_as_floats(k):
                dve.wait_ge(topi_ready, k + 1)
                nc.vector.tensor_copy(topf[:, :, :], topi[:, :, 0:2]).then_inc(topf_ready, 1)

            def mark_experts(k):
                dve.wait_ge(topf_ready, k + 1)
                for hit, n in ((hit1, 0), (hit2, 1)):
                    last = nc.vector.tensor_tensor(
                        hit[:, :].rearrange("p (t e) -> p t e", e=NE), over_blocks(expert_no, NE),
                        topf[:, :, n:n + 1].to_broadcast([P, T, NE]), ALU.is_equal)
                last.then_inc(hits_ready, 1)

            def gate_sum(k):
                dve.wait_ge(egap_ready, k + 1)
                nc.vector.tensor_scalar(gden[:, :], egap[:, :], 1.0, None, ALU.add).then_inc(gden_ready, 1)

            def first_weight(k):
                dve.wait_ge(gden_ready, k + 1)
                nc.vector.reciprocal(wt1[:, :], gden[:, :]).then_inc(wt1_ready, 1)

            def second_weight(k):
                dve.wait_ge(wt1_ready, k + 1)
                nc.vector.tensor_tensor(wt2[:, :], egap[:, :], wt1[:, :], ALU.mult).then_inc(wt2_ready, 1)

            def weigh_marks(k):
                dve.wait_ge(hits_ready, k + 1)
                dve.wait_ge(wt2_ready, k + 1)
                nc.vector.tensor_tensor(experts(gat1), experts(hit1), per_block(wt1, NE), ALU.mult)
                nc.vector.tensor_tensor(experts(gat2), experts(hit2), per_block(wt2, NE),
                                        ALU.mult).then_inc(gats_ready, 1)

            def sum_gates(k):
                dve.wait_ge(gats_ready, k + 1)
                wait(dve, spread_ready, k)
                nc.vector.tensor_tensor(gates[:, :], gat1[:, :], gat2[:, :], ALU.add).then_inc(gates_ready, 1)

            def gate_chunk(s, par, q):
                dve.wait_ge(relu_done, STEP * s + q + 1)
                wait(dve, y_pairs, STEP // 2 * s + (q - GRING) // 2 + 1)
                if q % CHUNKS == 0:
                    dve.wait_ge(g_copied, 2 * s + q // CHUNKS + 1)
                nc.vector.tensor_tensor(hg[q % GRING][:, :], ps[q % SRING][:, :], gt[par][:, tile_of(q)],
                                        ALU.mult).then_inc(gated_dve, 1)

            def add_ffn(k, par):
                dve.wait_ge(f_done, k + 1)
                dve.wait_ge(xk_ready, k + 1)
                wait(dve, cen3_ready, k)
                nc.vector.tensor_tensor(ysum[:, :], pf[:, :], xk[par][:, :], ALU.add).then_inc(ysum_ready, 1)

            def sums_last(k):
                dve.wait_ge(ysum_ready, k + 1)
                nc.vector.tensor_reduce(sum3[:, :], blocks(ysum), AX_X, ALU.add).then_inc(sum3_ready, 1)

            def divide_last(k):
                dve.wait_ge(sum3_ready, k + 1)
                nc.vector.tensor_scalar(mean3[:, :], sum3[:, :], 1.0 / C, None,
                                        ALU.mult).then_inc(mean3_ready, 1)

            def squares_last(k):
                dve.wait_ge(sq3_ready, k + 1)
                wait(dve, std3_ready, k)
                nc.vector.tensor_reduce(ss3[:, :], blocks(sq3), AX_X, ALU.add).then_inc(ss3_ready, 1)

            def invert_last(k):
                dve.wait_ge(std3_ready, k + 1)
                nc.vector.reciprocal(rstd3[:, :], std3[:, :]).then_inc(rstd3_ready, 1)

            def scale_last(k):
                dve.wait_ge(rstd3_ready, k + 1)
                dve.wait_ge(cen3_ready, k + 1)
                wait(dve, yg_ready, k)
                nc.vector.tensor_tensor(blocks(yn), blocks(cen3), per_block(rstd3),
                                        ALU.mult).then_inc(yn_ready, 1)

            def step(s, par):
                for q in range(STEP):
                    if has(s) and not on_pool(q):
                        gate_chunk(s, par, q)
                    if q == 0 and has(s + 2):
                        token_squares(s + 2)
                    if q == 3 and has(s + 2):
                        token_scale(s + 2, par)
                    if q == 4 and has(s + 2):
                        scale_head_std(s + 2, par)
                    if q == 5 and has(s + 2):
                        add_eps(s + 2)
                    if q == 6 and has(s + 2):
                        invert_heads(s + 2)
                    if q == 7 and has(s + 2):
                        head_factors(s + 2, par)
                    if q == 13 and has(s + 2):
                        normalise_heads(s + 2)
                    if q == 18 and has(s + 2):
                        copy_m(s + 2)
                    if q == 22 and has(s + 2):
                        attention_matrix(s + 2)
                    if q == 23 and has(s + 2):
                        add_identity(s + 2)
                    if q == 27 and has(s + 2):
                        scale_attention(s + 2, par)
                    if q == 23 and has(s + 3):
                        add_position(s + 3, 1 - par)
                    if q == 24 and has(s + 3):
                        head_sums(s + 3, 1 - par)
                    if q == 25 and has(s + 3):
                        token_sums(s + 3)
                    if q == 26 and has(s + 3):
                        token_mean(s + 3)
                        center_heads(s + 3, 1 - par)
                    if q == 28 and has(s + 3):
                        head_offsets(s + 3)
                    if q == 29 and has(s + 3):
                        square_offsets(s + 3)
                        head_squares(s + 3)
                    if q == 31 and has(s + 3):
                        token_parts(s + 3)
                    if q == 30 and has(s + 2):
                        statistics(s + 2)
                    if q == 31 and has(s + 2):
                        aggregate(s + 2)
                    if q == 1 and has(s + 1):
                        scale_again(s + 1)
                    if q == 7 and has(s + 1):
                        split_lo(s + 1, 1 - par, 0)
                    if q == 8 and has(s + 1):
                        split_lo(s + 1, 1 - par, 1)
                    if q == 11 and has(s + 1):
                        add_gate_bias(s + 1)
                    if q == 12 and has(s + 1):
                        add_hi_part(s + 1)
                        top_values(s + 1)
                    if q == 13 and has(s + 1):
                        top_gap(s + 1)
                    if q == 14 and has(s + 1):
                        top_places(s + 1)
                    if q == 15 and has(s + 1):
                        places_as_floats(s + 1)
                    if q == 16 and has(s + 1):
                        mark_experts(s + 1)
                    if q == 17 and has(s + 1):
                        gate_sum(s + 1)
                    if q == 18 and has(s + 1):
                        first_weight(s + 1)
                    if q == 19 and has(s + 1):
                        second_weight(s + 1)
                    if q == 20 and has(s + 1):
                        weigh_marks(s + 1)
                    if q == 21 and has(s + 1):
                        sum_gates(s + 1)
                    if q == 9 and has(s - 1):
                        add_ffn(s - 1, 1 - par)
                    if q == 10 and has(s - 1):
                        sums_last(s - 1)
                    if q == 11 and has(s - 1):
                        divide_last(s - 1)
                    if q == 15 and has(s - 1):
                        squares_last(s - 1)
                    if q == 18 and has(s - 1):
                        invert_last(s - 1)
                    if q == 19 and has(s - 1):
                        scale_last(s - 1)

            pipeline(dve, step)

        @block.tensor
        def _(pe):
            pe.wait_ge(const_in, ALL_CONSTS)
            pe.wait_ge(b2_in, 16)
            pe.wait_ge(weights_ready, 5)
            pe.wait_ge(ones_ready, 2)

            def embed_patches(k, par):
                pe.wait_ge(loaded, 16 * (k + 1))
                wait(pe, ht_copied, 2 * k)
                wait(pe, ysum_ready, k - 3)
                for t in range(T):
                    last = nc.tensor.matmul(pf[:, t * C:(t + 1) * C], xin[par][:, t * P:(t + 1) * P],
                                            wt[:, :], start=True, stop=True)
                last.then_inc(embedded, 1)

            def turn_tokens(k, half):
                pe.wait_ge(hcen_ready, k + 1)
                if half == 0:
                    wait(pe, lo_ready, 2 * k)
                else:
                    pe.wait_ge(h_ready, k + 1)
                    wait(pe, g_copied, 2 * (k - 1))
                    wait(pe, ysum_ready, k - 2)
                settle(pe, "pe")
                for t in range(TT):
                    b = half * TT + t
                    last = nc.tensor.transpose((pa, pf)[half][0:C, t * P:(t + 1) * P], hcen[:, b * C:(b + 1) * C],
                                               eye[:, :])
                last.then_inc(ht_turned, 1)

            def gram(k):
                pe.wait_ge(n_ready, k + 1)
                pe.wait_ge(ht_copied, 2 * k + 2)
                for t in range(T):
                    last = nc.tensor.matmul(pa[0:C + 1, 0:C + 1], naug[:, t, :], naug[:, t, :],
                                            start=(t == 0), stop=(t == T - 1))
                last.then_inc(m_done, 1)

            def times_v(k):
                pe.wait_ge(m_copied, k + 1)
                nc.tensor.matmul(pa[0:C + 1, 128:128 + C], maug[:, :], vaug[:, :], start=True,
                                 stop=True).then_inc(t_done, 1)

            def times_k(k):
                pe.wait_ge(t_copied, k + 1)
                nc.tensor.matmul(pa[0:C, 256:256 + C], kaug[:, :], tm[:, :], start=True,
                                 stop=True).then_inc(kv_done, 1)

            def attention(k):
                pe.wait_ge(am_ready, k + 1)
                pe.wait_ge(am0_ready, k + 1)
                for t in range(T):
                    last = nc.tensor.matmul(pa[:, t * C:(t + 1) * C], ht[:, t * P:(t + 1) * P], am[:, :],
                                            start=True, stop=True)
                last.then_inc(attended, 1)

            def turn_x(k, half):
                pe.wait_ge(xn_ready, k + 1)
                if half == 0:
                    wait(pe, g_copied, 2 * k)
                else:
                    pe.wait_ge(osc_ready, k + 1)
                settle(pe, "pe")
                for t in range(TT):
                    b = half * TT + t
                    last = nc.tensor.transpose((pb, pa)[half][0:C, t * P:(t + 1) * P], xn[:, b * C:(b + 1) * C],
                                               eye[:, :])
                last.then_inc(x_turned, 1)

            def gate_logits(k, par):
                pe.wait_ge(lo_ready, 2 * k + 2)
                for t in range(T):
                    last = nc.tensor.matmul(pb[:, 2 * t * NE:2 * (t + 1) * NE],
                                            xs[par][:, t * P:(t + 1) * P], gwr[:, :],
                                            start=True, stop=True)
                last.then_inc(logits_done, 1)

            def turn_gates(k, half):
                pe.wait_ge(spread_ready, k + 1)
                if half == 0:
                    pe.wait_ge(logit_ready, k + 1)
                else:
                    pe.wait_ge(h_ready, min(k + 3, B) if isinstance(k, int) else k + 3)
                for t in range(TT):
                    b = half * TT + t
                    last = nc.tensor.transpose((pb, pf)[half][:, t * P:(t + 1) * P], spread[:, b * P:(b + 1) * P],
                                               eye[:, :])
                last.then_inc(g_turned, 1)

            def hidden(s, par, q):
                c = q % CHUNKS
                if on_pool(q):
                    wait(pe, relu_done, STEP * s + q - SRING + 1)
                else:
                    wait(pe, gated_dve, DVE_STEP * s + (dve_gated(q - SRING) if q >= SRING else
                                                        dve_gated(q - SRING + STEP) - DVE_STEP))
                if q % CHUNKS == 0:
                    pe.wait_ge(lo_ready, 2 * s + q // CHUNKS + 1)
                nc.tensor.matmul(ps[q % SRING][:, :], w1h[:, c * P:(c + 1) * P], xs[par][:, tile_of(q)],
                                 start=True, stop=False)
                nc.tensor.matmul(ps[q % SRING][:, :], w1l[:, c * P:(c + 1) * P], xs[par][:, tile_of(q)],
                                 start=False, stop=True).then_inc(s_done, 1)

            def combine(s, q):
                first, final = q % CHUNKS == 0, q % CHUNKS == CHUNKS - 2
                pe.wait_ge(gated_dve, DVE_STEP * s + dve_gated(q + 1))
                if on_pool(q + 1):
                    pe.wait_ge(gated_pool, POOL_STEP * s + pool_gated(q + 1))
                if first:
                    wait(pe, y_copied, TILES * s + q // CHUNKS)
                for half in range(2):
                    c = (q + half) % CHUNKS
                    last = nc.tensor.matmul(py[half * C:(half + 1) * C, :], w2s[:, c * C:(c + 1) * C],
                                            hg[(q + half) % GRING][:, :], start=first, stop=final,
                                            skip_group_check=True)
                last.then_inc(y_pairs, 1)

            def tokens_again(k, par):
                pe.wait_ge(y_copied, TILES * (k + 1))
                pe.wait_ge(g_copied, min(2 * k + 4, 2 * B) if isinstance(k, int) else 2 * k + 4)
                for b in range(T):
                    tile, t = b // TT, b % TT
                    nc.tensor.matmul(pf[:, b * C:(b + 1) * C], yt[tile][:, t * P:(t + 1) * P], eye2[:, :],
                                     start=True, stop=False)
                    last = nc.tensor.matmul(pf[:, b * C:(b + 1) * C], gt[par][:, b * P:(b + 1) * P],
                                            b2x[:, :], start=False, stop=True)
                last.then_inc(f_done, 1)

            def step(s, par):
                for q in range(STEP):
                    if has(s):
                        hidden(s, par, q)
                    if q == GROUP - 1 and has(s - 1):
                        for pair in range(STEP - GROUP, STEP, 2):
                            combine(s - 1, pair)
                    if q % GROUP == GROUP - 1 and q >= GROUP and has(s):
                        for pair in range(q + 1 - 2 * GROUP, q + 1 - GROUP, 2):
                            combine(s, pair)
                    if q == 8 and has(s - 1):
                        tokens_again(s - 1, 1 - par)
                    if q == 8 and has(s + 1):
                        turn_x(s + 1, 0)
                        turn_x(s + 1, 1)
                    if q == 12 and has(s + 1):
                        gate_logits(s + 1, 1 - par)
                    if q == 13 and has(s + 2):
                        turn_tokens(s + 2, 0)
                        turn_tokens(s + 2, 1)
                    if q == 19 and has(s + 2):
                        gram(s + 2)
                    if q == 22 and has(s + 2):
                        times_v(s + 2)
                    if q == 24 and has(s + 2):
                        times_k(s + 2)
                    if q == 24 and has(s + 3):
                        embed_patches(s + 3, 1 - par)
                    if q == 28 and has(s + 2):
                        attention(s + 2)
                    if q == 28 and has(s + 1):
                        turn_gates(s + 1, 0)
                        turn_gates(s + 1, 1)

            pipeline(pe, step)


def kernel(x, L0_tok_W, L0_tok_b, L0_tok_pos_embed, L0_attn_kln_weight, L0_attn_kln_bias,
           L0_attn_vln_weight, L0_attn_vln_bias, L0_ffn_gate_w, L0_ffn_gate_b, L0_ffn_w1, L0_ffn_b1,
           L0_ffn_w2, L0_ffn_b2, L0_ffn_gamma, L0_ffn_beta):
    import numpy as np
    import concourse.bacc as bacc
    from concourse.bass_utils import run_bass_kernel_spmd

    patches = np.asarray(x).reshape(B, 16, 8, 64, 8).transpose(0, 2, 4, 1, 3).reshape(B, C, P, T)
    w1 = np.asarray(L0_ffn_w1).reshape(NE, C, CHUNKS, UN).transpose(1, 2, 0, 3).reshape(C, CHUNKS * P)
    w2 = np.asarray(L0_ffn_w2).reshape(NE, CHUNKS, UN, C).transpose(0, 2, 1, 3).reshape(P, CHUNKS * C)
    b1 = np.asarray(L0_ffn_b1).reshape(NE, CHUNKS, UN).transpose(0, 2, 1).reshape(P, CHUNKS)
    head = np.arange(C) // HD
    numbers = np.zeros((P, NE + T), np.float32)
    numbers[:, :NE] = np.arange(NE)
    numbers[:, NE:] = np.e
    arrays = {
        "patches": patches.transpose(0, 1, 3, 2).reshape(B, C, N),
        "tok_w": np.asarray(L0_tok_W).T,
        "tok_b": L0_tok_b,
        "pos": np.asarray(L0_tok_pos_embed).reshape(P, T * C),
        "k_w": np.asarray(L0_attn_kln_weight).reshape(C),
        "k_b": np.asarray(L0_attn_kln_bias).reshape(C),
        "v_w": np.asarray(L0_attn_vln_weight).reshape(C),
        "v_b": np.asarray(L0_attn_vln_bias).reshape(C),
        "gate_w": L0_ffn_gate_w,
        "gate_b": L0_ffn_gate_b,
        "w1": w1,
        "b1": b1,
        "w2": w2,
        "b2": L0_ffn_b2,
        "gamma": L0_ffn_gamma,
        "beta": L0_ffn_beta,
        "ident": np.eye(P, dtype=np.float32),
        "head_mask": (head[:, None] == head[None, :]).astype(np.float32) / np.float32(N),
        "numbers": numbers,
    }
    nc = bacc.Bacc("TRN2", target_bir_lowering=False, num_devices=1)
    given, args = {}, []
    for name, a in arrays.items():
        a = np.ascontiguousarray(a)
        given[f"in_{name}"] = a
        args.append(nc.dram_tensor(f"in_{name}", a.shape, mybir.dt.from_np(a.dtype),
                                   kind="ExternalInput").ap())
    out = nc.dram_tensor("out", (B, P, T * C), F32, kind="ExternalOutput").ap()
    tower(nc, *args, out)
    r = run_bass_kernel_spmd(nc, [given], core_ids=[0])
    return r.results[0]["out"].reshape(B, N, C)
```

```python
from contextlib import ExitStack

import concourse.bass as bass
from concourse import mybir

F32 = mybir.dt.float32
F32R = mybir.dt.float32r
U32 = mybir.dt.uint32
ALU = mybir.AluOpType
ACT = mybir.ActivationFunctionType
AX_X = mybir.AxisListType.X

P = 128
B = 16
N = 1024
T = N // P
C = 64
HEADS = 8
HD = C // HEADS
GROUPS = T * HEADS
NE = 16
FH = 128
UN = P // NE
CHUNKS = FH // UN
W = 512
TILES = N // W
TT = W // P
STEP = CHUNKS * TILES
SRING = 4
GRING = 8
GROUP = 4
EPS = 1e-5


def on_pool(chunk):
    return chunk % 4 == 3


def dve_gated(chunk):
    return chunk // 4 * 3 + min(chunk % 4 + 1, 3)


def pool_gated(chunk):
    return (chunk + 1) // 4


DVE_STEP = dve_gated(STEP - 1)
POOL_STEP = pool_gated(STEP - 1)


def has(batch):
    return not isinstance(batch, int) or 0 <= batch < B


def tower(nc, patches, tok_w, pos, vectors, kv_weight, kv_bias, per_row, w1, w2, b2, fixed, out):
    with ExitStack() as ctx:
        def sb(name, shape, dt=F32):
            return ctx.enter_context(nc.sbuf_tensor(name, shape, dt))

        def sem(name):
            return ctx.enter_context(nc.semaphore(name))

        fixed_sb = sb("fixed_sb", [P, 2 * P + NE + T])
        eye = fixed_sb[:, 0:P]
        mask_n = fixed_sb[:, P:2 * P]
        expert_no = fixed_sb[:, 2 * P:2 * P + NE]
        euler = fixed_sb[:, 2 * P + NE:2 * P + NE + T]
        wt = sb("wt", [P, 2 * C])
        posb = sb("posb", [P, T * C])
        vectors_sb = sb("vectors_sb", [P, 3 * C + NE])
        tokb = vectors_sb[:, 0:C]
        gam = vectors_sb[:, C:2 * C]
        bet = vectors_sb[:, 2 * C:3 * C]
        gbias = vectors_sb[:, 3 * C:3 * C + NE]
        kvaug = sb("kvaug", [C + 1, 3 * C])
        kaug = kvaug[:, 0:2 * C]
        vaug = kvaug[:, 2 * C:3 * C]
        kwv = sb("kwv", [C, 2])
        per_row_sb = sb("per_row_sb", [P, NE + CHUNKS])
        gw2 = per_row_sb[:, 0:NE]
        b1s = per_row_sb[:, NE:NE + CHUNKS]
        gwr = sb("gwr", [P, 2 * NE], F32R)
        w1f = sb("w1f", [P, CHUNKS * P])
        w1h = sb("w1h", [P, CHUNKS * P], F32R)
        w1l = sb("w1l", [P, CHUNKS * P], F32R)
        w2s = sb("w2s", [P, CHUNKS * C])
        b2x = sb("b2x", [P, C])
        epsc = sb("epsc", [P, 1])
        xin = [sb(f"xin{i}", [P, W]) for i in range(2)]
        h = [sb(f"h{i}", [P, T * C]) for i in range(2)]
        rstd1 = [sb(f"rstd1{i}", [P, T]) for i in range(2)]
        hsum = sb("hsum", [P, GROUPS])
        hmean = sb("hmean", [P, GROUPS])
        sum1 = sb("sum1", [P, T])
        mean1 = sb("mean1", [P, T])
        off = sb("off", [P, GROUPS])
        off2 = sb("off2", [P, GROUPS])
        hc = sb("hc", [P, T * C])
        sq1 = sb("sq1", [P, T * C])
        hss = sb("hss", [P, GROUPS])
        tss = sb("tss", [P, GROUPS])
        ss1 = sb("ss1", [P, T])
        std1 = sb("std1", [P, T])
        hstd = sb("hstd", [P, GROUPS])
        den = sb("den", [P, GROUPS])
        den2 = sb("den2", [P, GROUPS])
        rden = sb("rden", [P, GROUPS])
        fac = sb("fac", [P, GROUPS])
        naug = sb("naug", [P, T, C + 1])
        hcen = sb("hcen", [P, T * C])
        ht = sb("ht", [P, W])
        maug = sb("maug", [C + 1, C + 1])
        tm = sb("tm", [C + 1, C])
        am0 = sb("am0", [P, 2 * C])
        am = sb("am", [P, 2 * C])
        osc = sb("osc", [P, T * C])
        h2 = sb("h2", [P, T * C])
        halves = sb("halves", [P, T, 6])
        stats2 = sb("stats2", [P, T, 2])
        cen2 = sb("cen2", [P, T * C])
        std2 = sb("std2", [P, T])
        rstd2 = sb("rstd2", [P, T])
        xn = sb("xn", [P, T * C])
        xk = [sb(f"xk{i}", [P, T * C]) for i in range(2)]
        hb = [sb(f"hb{i}", [P, T * C]) for i in range(2)]
        xs = [sb(f"xs{i}", [P, N], F32R) for i in range(2)]
        part = sb("part", [P, T * NE])
        logit = sb("logit", [P, T * NE])
        top = sb("top", [P, T, 8])
        topi = sb("topi", [P, T, 8], U32)
        topf = sb("topf", [P, T, 2])
        gap = sb("gap", [P, T])
        egap = sb("egap", [P, T])
        gden = sb("gden", [P, T])
        wt1 = sb("wt1", [P, T])
        wt2 = sb("wt2", [P, T])
        hit1 = sb("hit1", [P, T * NE])
        hit2 = sb("hit2", [P, T * NE])
        gat1 = sb("gat1", [P, T * NE])
        gat2 = sb("gat2", [P, T * NE])
        gates = sb("gates", [P, T * NE])
        spread = sb("spread", [P, N])
        gt = [sb(f"gt{i}", [P, N]) for i in range(2)]
        rl = [sb(f"rl{i}", [P, W]) for i in range(2)]
        hg = [sb(f"hg{i}", [P, W]) for i in range(GRING)]
        ya = sb("ya", [P, W])
        yb = sb("yb", [P, W])
        yt = sb("yt", [P, W])
        ysum = sb("ysum", [P, T * C])
        sum3 = sb("sum3", [P, T])
        mean3 = sb("mean3", [P, T])
        cen3 = sb("cen3", [P, T * C])
        sq3 = sb("sq3", [P, T * C])
        ss3 = sb("ss3", [P, T])
        std3 = sb("std3", [P, T])
        rstd3 = sb("rstd3", [P, T])
        yn = sb("yn", [P, T * C])
        yg = sb("yg", [P, T * C])
        res = sb("res", [P, T * C])

        ps = [ctx.enter_context(nc.psum_tensor(f"ps{i}", [P, W], F32)) for i in range(SRING)]
        py = ctx.enter_context(nc.psum_tensor("py", [P, W], F32))
        pf = ctx.enter_context(nc.psum_tensor("pf", [P, W], F32))
        pa = ctx.enter_context(nc.psum_tensor("pa", [P, W], F32))
        pb = ctx.enter_context(nc.psum_tensor("pb", [P, W], F32))

        embed_in, ffn_in = sem("embed_in"), sem("ffn_in")
        sparse_in = sem("sparse_in")
        hi_weights, ffn_weights, embed_weights, ones_ready, zero_ready = (
            sem(x) for x in ("hi_weights", "ffn_weights", "embed_weights", "ones_ready", "zero_ready"))
        loaded, stored = sem("loaded"), sem("stored")
        embedded, h_ready, sums_ready, hmean_ready, mean1_ready, off_ready, off2_ready = (
            sem(x) for x in ("embedded", "h_ready", "sums_ready", "hmean_ready", "mean1_ready",
                             "off_ready", "off2_ready"))
        sum1_ready, hc_ready, sq1_ready, hss_ready, tss_ready, ss1_ready, std1_ready, hstd_ready = (
            sem(x) for x in ("sum1_ready", "hc_ready", "sq1_ready", "hss_ready", "tss_ready",
                             "ss1_ready", "std1_ready", "hstd_ready"))
        rstd1_ready, den_ready, den2_ready, rden_ready, fac_ready, n_ready, hcen_ready = (
            sem(x) for x in ("rstd1_ready", "den_ready", "den2_ready", "rden_ready", "fac_ready",
                             "n_ready", "hcen_ready"))
        ht_turned, ht_copied = sem("ht_turned"), sem("ht_copied")
        m_done, m_copied, t_done, t_copied, kv_done, am0_ready, am_ready = (
            sem(x) for x in ("m_done", "m_copied", "t_done", "t_copied", "kv_done", "am0_ready",
                             "am_ready"))
        attended, osc_ready, h2_ready, halves_ready, stats_ready, cen2_ready = (
            sem(x) for x in ("attended", "osc_ready", "h2_ready", "halves_ready", "stats_ready",
                             "cen2_ready"))
        std2_ready, rstd2_ready, xn_ready, xk_ready, hb_ready = (
            sem(x) for x in ("std2_ready", "rstd2_ready", "xn_ready", "xk_ready", "hb_ready"))
        x_turned, hi_ready, lo_ready = sem("x_turned"), sem("hi_ready"), sem("lo_ready")
        logits_done, logit_ready, top_ready, topi_ready, topf_ready, gap_ready, egap_ready = (
            sem(x) for x in ("logits_done", "logit_ready", "top_ready", "topi_ready", "topf_ready",
                             "gap_ready", "egap_ready"))
        gden_ready, wt1_ready, wt2_ready, hits_ready, gats_ready, gates_ready = (
            sem(x) for x in ("gden_ready", "wt1_ready", "wt2_ready", "hits_ready", "gats_ready",
                             "gates_ready"))
        spread_ready, part_ready = sem("spread_ready"), sem("part_ready")
        g_turned, g_copied = sem("g_turned"), sem("g_copied")
        s_done, relu_done = sem("s_done"), sem("relu_done")
        gated_dve, gated_pool = sem("gated_dve"), sem("gated_pool")
        y_pairs, y_copied, y_added, f_done = (
            sem(x) for x in ("y_pairs", "y_copied", "y_added", "f_done"))
        passed = {e: sem(f"passed_{e}") for e in ("pe", "dve", "sp")}
        ysum_ready, sum3_ready, mean3_ready, cen3_ready, sq3_ready, ss3_ready, std3_ready = (
            sem(x) for x in ("ysum_ready", "sum3_ready", "mean3_ready", "cen3_ready", "sq3_ready",
                             "ss3_ready", "std3_ready"))
        rstd3_ready, yn_ready, yg_ready, res_ready = (
            sem(x) for x in ("rstd3_ready", "yn_ready", "yg_ready", "res_ready"))

        def wait(eng, s, value):
            if not isinstance(value, int) or value > 0:
                eng.wait_ge(s, value)

        def tile_of(q):
            return slice(q // CHUNKS * W, (q // CHUNKS + 1) * W)

        def columns(b):
            return slice(b % 2 * W + b // 2 * P, b % 2 * W + (b // 2 + 1) * P)

        def settle(eng, name):
            eng.sem_inc(passed[name], 1)

        def blocks(buf):
            return buf[:, :].rearrange("p (t c) -> p t c", t=T)

        def heads(buf):
            return buf[:, :].rearrange("p (g d) -> p g d", d=HD)

        def per_block(small, n=C):
            return small[:, :].unsqueeze(2).to_broadcast([P, T, n])

        def per_head(small):
            return small[:, :].unsqueeze(2).to_broadcast([P, GROUPS, HD])

        def over_blocks(row, n=C):
            return row[:, :].unsqueeze(1).to_broadcast([P, T, n])

        def pipeline(eng, step):
            for s in range(-3, 2):
                step(s, s % 2)
            with eng.Fori(0, (B - 6) // 2) as i:
                step(2 * i + 2, 0)
                step(2 * i + 3, 1)
            for s in range(B - 4, B + 1):
                step(s, s % 2)

        block = ctx.enter_context(nc.Block())

        @block.sync
        def _(sp):
            def load_constants():
                for dst, src in ((posb, pos), (kwv, kv_weight)):
                    sp.dma_start(dst[:, :], src[:, :]).then_inc(embed_in, 16)
                sp.dma_start(kvaug[C:C + 1, :], kv_bias.unsqueeze(0)).then_inc(embed_in, 16)

            def load(k, par):
                wait(sp, loaded, 16 * k)
                settle(sp, "sp")
                wait(sp, embedded, k - 1)
                settle(sp, "sp")
                sp.dma_start(xin[par][:, :], patches[k, :, :] if isinstance(k, int)
                             else patches[bass.ds(k, 1), :, :].rearrange("a c n -> (a c) n")).then_inc(loaded, 16)

            def store(k):
                wait(sp, stored, 16 * k)
                settle(sp, "sp")
                sp.wait_ge(res_ready, k + 1)
                settle(sp, "sp")
                dst = out[k, :, :] if isinstance(k, int) else \
                    out[bass.ds(k, 1), :, :].rearrange("a p n -> (a p) n")
                sp.dma_start(dst, res[:, :]).then_inc(stored, 16)

            def step(s, par):
                if has(s + 3):
                    load(s + 3, 1 - par)
                if isinstance(s, int) and s == -3:
                    load_constants()
                if has(s - 1):
                    store(s - 1)

            pipeline(sp, step)
            sp.wait_ge(stored, 16 * B)

        @block.gpsimd
        def _(pool):
            nc.gpsimd.memset(wt[:, :], 0.0).then_inc(zero_ready, 1)
            nc.gpsimd.memset(b2x[:, :], 0.0).then_inc(zero_ready, 1)
            nc.gpsimd.memset(naug[:, :, C:C + 1], 1.0).then_inc(ones_ready, 1)
            nc.gpsimd.memset(epsc[:, :], EPS).then_inc(ones_ready, 1)
            pool.wait_ge(zero_ready, 2)
            pool.dma_start(wt[0:C, 0:C], tok_w[:, :]).then_inc(sparse_in, 16)
            pool.dma_start(wt[C:P, C:2 * C], tok_w[:, :]).then_inc(sparse_in, 16)
            pool.dma_start(b2x[0:P:UN, :], b2[:, :]).then_inc(sparse_in, 16)

            def low_weights():
                pool.wait_ge(hi_weights, 2)
                nc.gpsimd.tensor_tensor(w1l[:, :], w1f[:, :], w1h[:, :].bitcast(F32),
                                        ALU.subtract).then_inc(ffn_weights, 1)

            def center_tokens(k, par):
                pool.wait_ge(mean1_ready, k + 1)
                wait(pool, ht_turned, k)
                nc.gpsimd.tensor_tensor(blocks(hcen), blocks(h[par]), per_block(mean1),
                                        ALU.subtract).then_inc(hcen_ready, 1)

            def add_attention(k, par):
                pool.wait_ge(osc_ready, k + 1)
                wait(pool, hb_ready, k)
                nc.gpsimd.tensor_tensor(h2[:, :], osc[:, :], h[par][:, :], ALU.add).then_inc(h2_ready, 1)

            def center_again(k):
                pool.wait_ge(stats_ready, k + 1)
                pool.wait_ge(h2_ready, k + 1)
                wait(pool, xn_ready, k)
                nc.gpsimd.tensor_tensor(blocks(cen2), blocks(h2), stats2[:, :, 0:1].to_broadcast([P, T, C]),
                                        ALU.subtract).then_inc(cen2_ready, 1)

            def scale_again(k):
                pool.wait_ge(rstd2_ready, k + 1)
                pool.wait_ge(cen2_ready, k + 1)
                wait(pool, xk_ready, k)
                nc.gpsimd.tensor_tensor(blocks(xn), blocks(cen2), per_block(rstd2),
                                        ALU.mult).then_inc(xn_ready, 1)

            def exp_gap(k):
                pool.wait_ge(gap_ready, k + 1)
                wait(pool, wt2_ready, k)
                nc.gpsimd.tensor_tensor(egap[:, :], euler[:, :], gap[:, :], ALU.pow).then_inc(egap_ready, 1)

            def add_beta(k, par):
                pool.wait_ge(h2_ready, k + 1)
                wait(pool, res_ready, k - 1)
                nc.gpsimd.tensor_tensor(blocks(hb[par]), blocks(h2), over_blocks(bet),
                                        ALU.add).then_inc(hb_ready, 1)

            def add_halves(k):
                pool.wait_ge(y_copied, TILES * (k + 1))
                wait(pool, f_done, k)
                nc.gpsimd.tensor_tensor(yt[:, :], ya[:, :], yb[:, :], ALU.add).then_inc(y_added, 1)

            def center_last(k):
                pool.wait_ge(mean3_ready, k + 1)
                wait(pool, yn_ready, k)
                nc.gpsimd.tensor_tensor(blocks(cen3), blocks(ysum), per_block(mean3),
                                        ALU.subtract).then_inc(cen3_ready, 1)

            def times_gamma(k):
                pool.wait_ge(yn_ready, k + 1)
                nc.gpsimd.tensor_tensor(blocks(yg), blocks(yn), over_blocks(gam),
                                        ALU.mult).then_inc(yg_ready, 1)

            def add_residual(k, par):
                pool.wait_ge(yg_ready, k + 1)
                wait(pool, stored, 16 * k)
                nc.gpsimd.tensor_tensor(res[:, :], yg[:, :], hb[par][:, :], ALU.add).then_inc(res_ready, 1)

            def gate_chunk(s, par, q):
                pool.wait_ge(relu_done, STEP * s + q + 1)
                wait(pool, y_pairs, STEP // 2 * s + (q - GRING) // 2 + 1)
                if q % CHUNKS < 4:
                    pool.wait_ge(g_copied, 2 * s + q // CHUNKS + 1)
                nc.gpsimd.tensor_tensor(hg[q % GRING][:, :], rl[q // 4 % 2][:, :], gt[par][:, tile_of(q)],
                                        ALU.mult).then_inc(gated_pool, 1)

            def step(s, par):
                if isinstance(s, int) and s == -2:
                    low_weights()
                for q in range(STEP):
                    if has(s) and on_pool(q):
                        gate_chunk(s, par, q)
                    if q == 0 and has(s + 1):
                        center_again(s + 1)
                    if q == 4 and has(s + 1):
                        scale_again(s + 1)
                    if q == 4 and has(s - 1):
                        add_halves(s - 1)
                    if q == 14 and has(s - 1):
                        center_last(s - 1)
                    if q == 16 and has(s + 1):
                        exp_gap(s + 1)
                    if q == 20 and has(s - 1):
                        times_gamma(s - 1)
                    if q == 23 and has(s - 1):
                        add_residual(s - 1, 1 - par)
                    if q == 23 and has(s + 1):
                        add_beta(s + 1, 1 - par)
                    if q == 25 and has(s + 3):
                        center_tokens(s + 3, 1 - par)
                    if q == 29 and has(s + 2):
                        add_attention(s + 2, par)

            pipeline(pool, step)

        @block.scalar
        def _(act):
            act.dma_start(fixed_sb[:, :], fixed[:, :]).then_inc(embed_in, 16)
            act.dma_start(vectors_sb[:, :], vectors.unsqueeze(0).to_broadcast([P, 3 * C + NE])).then_inc(embed_in, 16)
            for dst, src in ((per_row_sb, per_row), (w1f, w1), (w2s, w2)):
                act.dma_start(dst[:, :], src[:, :]).then_inc(ffn_in, 16)
            act.wait_ge(ones_ready, 2)

            def round_weights():
                act.wait_ge(ffn_in, 3 * 16)
                nc.scalar.activation(gwr[:, 0:NE], gw2[:, :], ACT.Copy).then_inc(hi_weights, 1)
                nc.scalar.activation(w1h[:, :], w1f[:, :], ACT.Copy).then_inc(hi_weights, 1)

            def square_heads(k):
                act.wait_ge(hc_ready, k + 1)
                wait(act, hss_ready, k)
                nc.scalar.activation(sq1[:, :], hc[:, :], ACT.Square).then_inc(sq1_ready, 1)

            def roots(k):
                act.wait_ge(ss1_ready, k + 1)
                nc.scalar.activation(std1[:, :], ss1[:, :], ACT.Sqrt, bias=epsc[:, 0:1],
                                     scale=1.0 / C).then_inc(std1_ready, 1)
                nc.scalar.activation(hstd[:, :], hss[:, :], ACT.Sqrt,
                                     scale=1.0 / (HD - 1)).then_inc(hstd_ready, 1)

            def copy_ht(k):
                act.wait_ge(ht_turned, k + 1)
                wait(act, attended, k)
                nc.scalar.activation(ht[:, :], pa[:, :], ACT.Copy).then_inc(ht_copied, 1)

            def copy_t(k):
                act.wait_ge(t_done, k + 1)
                nc.scalar.activation(tm[:, :], pa[0:C + 1, 128:128 + C], ACT.Copy).then_inc(t_copied, 1)

            def root_again(k):
                act.wait_ge(stats_ready, k + 1)
                wait(act, rstd2_ready, k)
                nc.scalar.activation(std2[:, :], stats2[:, :, 1], ACT.Sqrt,
                                     bias=epsc[:, 0:1]).then_inc(std2_ready, 1)

            def keep_xn(k, par):
                act.wait_ge(xn_ready, k + 1)
                wait(act, ysum_ready, k - 1)
                nc.scalar.activation(xk[par][:, :], xn[:, :], ACT.Copy).then_inc(xk_ready, 1)

            def round_hi(k, par, half):
                rows = slice(half * C, (half + 1) * C)
                act.wait_ge(x_turned, k + 1)
                nc.scalar.activation(xs[par][rows, half * W:(half + 1) * W], pb[rows, :],
                                     ACT.Copy).then_inc(hi_ready, 1)

            def spread_gates(k):
                act.wait_ge(gates_ready, k + 1)
                wait(act, g_turned, 2 * k)
                nc.scalar.activation(spread[:, :].rearrange("p (g u) -> p g u", u=UN),
                                     gates[:, :].unsqueeze(2).to_broadcast([P, T * NE, UN]),
                                     ACT.Copy).then_inc(spread_ready, 1)

            def copy_gates(k, par, half):
                act.wait_ge(g_turned, 2 * k + half + 1)
                wait(act, f_done, k - 1)
                nc.scalar.activation(gt[par][:, half * W:(half + 1) * W], (pb, pf)[half][:, :],
                                     ACT.Copy).then_inc(g_copied, 1)

            def copy_y(k, tile):
                act.wait_ge(y_pairs, STEP // 2 * k + CHUNKS // 2 * (tile + 1))
                wait(act, y_added, k)
                rows = slice(tile * C, (tile + 1) * C)
                nc.scalar.activation(ya[rows, :], py[0:C, :], ACT.Copy)
                nc.scalar.activation(yb[rows, :], py[C:P, :], ACT.Copy).then_inc(y_copied, 1)

            def square_last(k):
                act.wait_ge(cen3_ready, k + 1)
                wait(act, ss3_ready, k)
                nc.scalar.activation(sq3[:, :], cen3[:, :], ACT.Square).then_inc(sq3_ready, 1)

            def root_last(k):
                act.wait_ge(ss3_ready, k + 1)
                nc.scalar.activation(std3[:, :], ss3[:, :], ACT.Sqrt, bias=epsc[:, 0:1],
                                     scale=1.0 / C).then_inc(std3_ready, 1)

            def relu(s, q):
                act.wait_ge(s_done, STEP * s + q + 1)
                if on_pool(q):
                    wait(act, gated_pool, POOL_STEP * s + pool_gated(q) - 2)
                dst = rl[q // 4 % 2] if on_pool(q) else ps[q % SRING]
                c = q % CHUNKS
                nc.scalar.activation(dst[:, :], ps[q % SRING][:, :], ACT.Relu,
                                     bias=b1s[:, c:c + 1]).then_inc(relu_done, 1)

            def step(s, par):
                for q in range(STEP):
                    if has(s):
                        relu(s, q)
                    if q == 2 and has(s + 1):
                        root_again(s + 1)
                    if q == 5 and has(s + 2):
                        roots(s + 2)
                    if q == 14 and isinstance(s, int) and s == -2:
                        round_weights()
                    if q == GROUP - 1 and has(s - 1):
                        copy_y(s - 1, 1)
                    if q == 7 and has(s + 1):
                        round_hi(s + 1, 1 - par, 0)
                    if q == 10 and has(s + 1):
                        round_hi(s + 1, 1 - par, 1)
                    if q == 12 and has(s + 2):
                        copy_ht(s + 2)
                    if q == 14 and has(s - 1):
                        square_last(s - 1)
                    if q == 16 and has(s - 1):
                        root_last(s - 1)
                    if q == CHUNKS + GROUP - 1 and has(s):
                        copy_y(s, 0)
                    if q == 19 and has(s + 2):
                        copy_t(s + 2)
                    if q == 22 and has(s + 1):
                        keep_xn(s + 1, 1 - par)
                    if q == 25 and has(s + 1):
                        spread_gates(s + 1)
                    if q == 26 and has(s + 1):
                        copy_gates(s + 1, 1 - par, 0)
                    if q == 27 and has(s + 1):
                        copy_gates(s + 1, 1 - par, 1)
                    if q == 27 and has(s + 3):
                        square_heads(s + 3)

            pipeline(act, step)

        @block.vector
        def _(dve):
            dve.wait_ge(embed_in, 5 * 16)
            nc.vector.tensor_tensor(blocks(posb), blocks(posb), over_blocks(tokb),
                                    ALU.add).then_inc(embed_weights, 1)
            nc.vector.tensor_scalar(kaug[0:C, :].rearrange("p (n c) -> p n c", n=2),
                                    eye[0:C, 0:C].unsqueeze(1).to_broadcast([C, 2, C]), kwv[:, 0:1], None,
                                    ALU.mult).then_inc(embed_weights, 1)
            nc.vector.tensor_scalar(vaug[0:C, :], eye[0:C, 0:C], kwv[:, 1:2], None,
                                    ALU.mult).then_inc(embed_weights, 1)
            dve.wait_ge(embed_weights, 3)

            def low_gate_weights():
                dve.wait_ge(hi_weights, 1)
                nc.vector.tensor_tensor(gwr[:, NE:2 * NE], gw2[:, :], gwr[:, 0:NE].bitcast(F32),
                                        ALU.subtract).then_inc(ffn_weights, 1)

            def add_position(k, par):
                dve.wait_ge(embedded, k + 1)
                wait(dve, h2_ready, k - 1)
                nc.vector.tensor_tensor(h[par][:, :], pf[:, :], posb[:, :], ALU.add).then_inc(h_ready, 1)

            def head_sums(k, par):
                dve.wait_ge(h_ready, k + 1)
                nc.vector.tensor_reduce(hsum[:, :], heads(h[par]), AX_X, ALU.add).then_inc(sums_ready, 1)

            def token_sums(k):
                dve.wait_ge(sums_ready, k + 1)
                wait(dve, hcen_ready, k)
                nc.vector.tensor_reduce(sum1[:, :], hsum[:, :].rearrange("p (t g) -> p t g", g=HEADS),
                                        AX_X, ALU.add).then_inc(sum1_ready, 1)
                nc.vector.tensor_scalar(hmean[:, :], hsum[:, :], 1.0 / HD, None,
                                        ALU.mult).then_inc(hmean_ready, 1)

            def token_mean(k):
                dve.wait_ge(sum1_ready, k + 1)
                nc.vector.tensor_scalar(mean1[:, :], sum1[:, :], 1.0 / C, None,
                                        ALU.mult).then_inc(mean1_ready, 1)

            def center_heads(k, par):
                dve.wait_ge(hmean_ready, k + 1)
                nc.vector.tensor_tensor(heads(hc), heads(h[par]), per_head(hmean),
                                        ALU.subtract).then_inc(hc_ready, 1)

            def head_offsets(k):
                dve.wait_ge(mean1_ready, k + 1)
                nc.vector.tensor_tensor(off[:, :].rearrange("p (t g) -> p t g", g=HEADS),
                                        hmean[:, :].rearrange("p (t g) -> p t g", g=HEADS),
                                        per_block(mean1, HEADS), ALU.subtract).then_inc(off_ready, 1)

            def square_offsets(k):
                dve.wait_ge(off_ready, k + 1)
                nc.vector.tensor_tensor(off2[:, :], off[:, :], off[:, :], ALU.mult).then_inc(off2_ready, 1)

            def head_squares(k):
                dve.wait_ge(sq1_ready, k + 1)
                wait(dve, hstd_ready, k)
                nc.vector.tensor_reduce(hss[:, :], heads(sq1), AX_X, ALU.add).then_inc(hss_ready, 1)

            def token_parts(k):
                dve.wait_ge(hss_ready, k + 1)
                dve.wait_ge(off2_ready, k + 1)
                nc.vector.scalar_tensor_tensor(tss[:, :], off2[:, :], float(HD), hss[:, :], ALU.mult,
                                               ALU.add).then_inc(tss_ready, 1)

            def token_squares(k):
                dve.wait_ge(tss_ready, k + 1)
                nc.vector.tensor_reduce(ss1[:, :], tss[:, :].rearrange("p (t g) -> p t g", g=HEADS),
                                        AX_X, ALU.add).then_inc(ss1_ready, 1)

            def groups(buf):
                return buf[:, :].rearrange("p (t g) -> p t g", g=HEADS)

            def token_scale(k, par):
                dve.wait_ge(std1_ready, k + 1)
                nc.vector.reciprocal(rstd1[par][:, :], std1[:, :]).then_inc(rstd1_ready, 1)

            def scale_head_std(k, par):
                dve.wait_ge(rstd1_ready, k + 1)
                dve.wait_ge(hstd_ready, k + 1)
                nc.vector.tensor_tensor(groups(den), groups(hstd), per_block(rstd1[par], HEADS),
                                        ALU.mult).then_inc(den_ready, 1)

            def add_eps(k):
                dve.wait_ge(den_ready, k + 1)
                nc.vector.tensor_scalar(den2[:, :], den[:, :], EPS, None, ALU.add).then_inc(den2_ready, 1)

            def invert_heads(k):
                dve.wait_ge(den2_ready, k + 1)
                nc.vector.reciprocal(rden[:, :], den2[:, :]).then_inc(rden_ready, 1)

            def head_factors(k, par):
                dve.wait_ge(rden_ready, k + 1)
                nc.vector.tensor_tensor(groups(fac), groups(rden), per_block(rstd1[par], HEADS),
                                        ALU.mult).then_inc(fac_ready, 1)

            def normalise_heads(k):
                dve.wait_ge(fac_ready, k + 1)
                wait(dve, m_done, k)
                nc.vector.tensor_tensor(
                    naug[:, :, 0:C].rearrange("p t (g d) -> p t g d", d=HD),
                    hc[:, :].rearrange("p (t g d) -> p t g d", g=HEADS, d=HD),
                    fac[:, :].rearrange("p (t g) -> p t g", g=HEADS).unsqueeze(3)
                    .to_broadcast([P, T, HEADS, HD]), ALU.mult).then_inc(n_ready, 1)

            def copy_m(k):
                dve.wait_ge(m_done, k + 1)
                nc.vector.tensor_copy(maug[:, :], pa[0:C + 1, 0:C + 1]).then_inc(m_copied, 1)

            def attention_matrix(k):
                dve.wait_ge(kv_done, k + 1)
                nc.vector.tensor_tensor(am0[:, :].rearrange("p (n c) -> p n c", n=2),
                                        pa[:, 256:256 + C].unsqueeze(1).to_broadcast([P, 2, C]),
                                        mask_n[:, :].rearrange("p (n c) -> p n c", n=2),
                                        ALU.mult).then_inc(am0_ready, 1)

            def add_identity(k):
                dve.wait_ge(am0_ready, k + 1)
                wait(dve, attended, k)
                nc.vector.tensor_tensor(am[:, :], am0[:, :], eye[:, :], ALU.add).then_inc(am_ready, 1)

            def scale_attention(k, par):
                dve.wait_ge(attended, k + 1)
                wait(dve, h2_ready, k)
                nc.vector.tensor_tensor(blocks(osc), blocks(pa), per_block(rstd1[par]),
                                        ALU.mult).then_inc(osc_ready, 1)

            def statistics(k, half):
                if half == 0:
                    dve.wait_ge(h2_ready, k + 1)
                    settle(dve, "dve")
                for t in range(half * TT, half * TT + TT):
                    last = nc.vector.bn_stats(halves[:, t, :], h2[:, t * C:(t + 1) * C])
                last.then_inc(halves_ready, 1)

            def aggregate(k):
                dve.wait_ge(halves_ready, 2 * k + 2)
                wait(dve, cen2_ready, k)
                wait(dve, std2_ready, k)
                settle(dve, "dve")
                for t in range(T):
                    last = nc.vector.bn_aggr(stats2[:, t, :], halves[:, t, :])
                last.then_inc(stats_ready, 1)

            def scale_again(k):
                dve.wait_ge(std2_ready, k + 1)
                wait(dve, xn_ready, k)
                nc.vector.reciprocal(rstd2[:, :], std2[:, :]).then_inc(rstd2_ready, 1)

            def split_lo(k, par, half):
                cols = slice(half * W, (half + 1) * W)
                rows, others = slice(half * C, (half + 1) * C), slice((1 - half) * C, (2 - half) * C)
                dve.wait_ge(hi_ready, 2 * k + half + 1)
                nc.vector.tensor_tensor(xs[par][others, cols], pb[rows, :], xs[par][rows, cols].bitcast(F32),
                                        ALU.subtract).then_inc(lo_ready, 1)

            def experts(buf):
                return buf[:, :].rearrange("p (t e) -> p t e", e=NE)

            def add_gate_bias(k):
                dve.wait_ge(logits_done, k + 1)
                both = pb[:, 0:2 * T * NE].rearrange("p (t n e) -> p t n e", n=2, e=NE)
                nc.vector.tensor_tensor(experts(part), both[:, :, 1, :], over_blocks(gbias, NE),
                                        ALU.add).then_inc(part_ready, 1)

            def add_hi_part(k):
                dve.wait_ge(part_ready, k + 1)
                both = pb[:, 0:2 * T * NE].rearrange("p (t n e) -> p t n e", n=2, e=NE)
                nc.vector.tensor_tensor(experts(logit), both[:, :, 0, :], experts(part),
                                        ALU.add).then_inc(logit_ready, 1)

            def top_values(k):
                dve.wait_ge(logit_ready, k + 1)
                settle(dve, "dve")
                for t in range(T):
                    last = nc.vector.max(top[:, t, :], logit[:, t * NE:(t + 1) * NE])
                last.then_inc(top_ready, 1)

            def top_gap(k):
                dve.wait_ge(top_ready, k + 1)
                wait(dve, egap_ready, k)
                nc.vector.tensor_tensor(gap[:, :], top[:, :, 1], top[:, :, 0],
                                        ALU.subtract).then_inc(gap_ready, 1)

            def top_places(k):
                dve.wait_ge(top_ready, k + 1)
                settle(dve, "dve")
                for t in range(T):
                    last = nc.vector.max_index(topi[:, t, :], top[:, t, :], logit[:, t * NE:(t + 1) * NE])
                last.then_inc(topi_ready, 1)

            def places_as_floats(k):
                dve.wait_ge(topi_ready, k + 1)
                nc.vector.tensor_copy(topf[:, :, :], topi[:, :, 0:2]).then_inc(topf_ready, 1)

            def mark_experts(k):
                dve.wait_ge(topf_ready, k + 1)
                for hit, n in ((hit1, 0), (hit2, 1)):
                    last = nc.vector.tensor_tensor(
                        hit[:, :].rearrange("p (t e) -> p t e", e=NE), over_blocks(expert_no, NE),
                        topf[:, :, n:n + 1].to_broadcast([P, T, NE]), ALU.is_equal)
                last.then_inc(hits_ready, 1)

            def gate_sum(k):
                dve.wait_ge(egap_ready, k + 1)
                nc.vector.tensor_scalar(gden[:, :], egap[:, :], 1.0, None, ALU.add).then_inc(gden_ready, 1)

            def first_weight(k):
                dve.wait_ge(gden_ready, k + 1)
                nc.vector.reciprocal(wt1[:, :], gden[:, :]).then_inc(wt1_ready, 1)

            def second_weight(k):
                dve.wait_ge(wt1_ready, k + 1)
                nc.vector.tensor_tensor(wt2[:, :], egap[:, :], wt1[:, :], ALU.mult).then_inc(wt2_ready, 1)

            def weigh_marks(k):
                dve.wait_ge(hits_ready, k + 1)
                dve.wait_ge(wt2_ready, k + 1)
                nc.vector.tensor_tensor(experts(gat1), experts(hit1), per_block(wt1, NE), ALU.mult)
                nc.vector.tensor_tensor(experts(gat2), experts(hit2), per_block(wt2, NE),
                                        ALU.mult).then_inc(gats_ready, 1)

            def sum_gates(k):
                dve.wait_ge(gats_ready, k + 1)
                wait(dve, spread_ready, k)
                nc.vector.tensor_tensor(gates[:, :], gat1[:, :], gat2[:, :], ALU.add).then_inc(gates_ready, 1)

            def gate_chunk(s, par, q):
                dve.wait_ge(relu_done, STEP * s + q + 1)
                wait(dve, y_pairs, STEP // 2 * s + (q - GRING) // 2 + 1)
                if q % CHUNKS == 0:
                    dve.wait_ge(g_copied, 2 * s + q // CHUNKS + 1)
                nc.vector.tensor_tensor(hg[q % GRING][:, :], ps[q % SRING][:, :], gt[par][:, tile_of(q)],
                                        ALU.mult).then_inc(gated_dve, 1)

            def add_ffn(k, par):
                dve.wait_ge(f_done, k + 1)
                dve.wait_ge(xk_ready, k + 1)
                wait(dve, cen3_ready, k)
                nc.vector.tensor_tensor(ysum[:, :], pf[:, :], xk[par][:, :], ALU.add).then_inc(ysum_ready, 1)

            def sums_last(k):
                dve.wait_ge(ysum_ready, k + 1)
                nc.vector.tensor_reduce(sum3[:, :], blocks(ysum), AX_X, ALU.add).then_inc(sum3_ready, 1)

            def divide_last(k):
                dve.wait_ge(sum3_ready, k + 1)
                nc.vector.tensor_scalar(mean3[:, :], sum3[:, :], 1.0 / C, None,
                                        ALU.mult).then_inc(mean3_ready, 1)

            def squares_last(k):
                dve.wait_ge(sq3_ready, k + 1)
                wait(dve, std3_ready, k)
                nc.vector.tensor_reduce(ss3[:, :], blocks(sq3), AX_X, ALU.add).then_inc(ss3_ready, 1)

            def invert_last(k):
                dve.wait_ge(std3_ready, k + 1)
                nc.vector.reciprocal(rstd3[:, :], std3[:, :]).then_inc(rstd3_ready, 1)

            def scale_last(k):
                dve.wait_ge(rstd3_ready, k + 1)
                dve.wait_ge(cen3_ready, k + 1)
                wait(dve, yg_ready, k)
                nc.vector.tensor_tensor(blocks(yn), blocks(cen3), per_block(rstd3),
                                        ALU.mult).then_inc(yn_ready, 1)

            def step(s, par):
                for q in range(STEP):
                    if has(s) and not on_pool(q):
                        gate_chunk(s, par, q)
                    if q == 16 and isinstance(s, int) and s == -2:
                        low_gate_weights()
                    if q == 2 and has(s + 2):
                        token_squares(s + 2)
                    if q == 3 and has(s + 2):
                        token_scale(s + 2, par)
                    if q == 4 and has(s + 2):
                        scale_head_std(s + 2, par)
                    if q == 5 and has(s + 2):
                        add_eps(s + 2)
                    if q == 6 and has(s + 2):
                        invert_heads(s + 2)
                    if q == 6 and has(s + 2):
                        head_factors(s + 2, par)
                    if q == 11 and has(s + 2):
                        normalise_heads(s + 2)
                    if q == 16 and has(s + 2):
                        copy_m(s + 2)
                    if q == 20 and has(s + 2):
                        attention_matrix(s + 2)
                    if q == 21 and has(s + 2):
                        add_identity(s + 2)
                    if q == 27 and has(s + 2):
                        scale_attention(s + 2, par)
                    if q == 24 and has(s + 3):
                        add_position(s + 3, 1 - par)
                    if q == 24 and has(s + 3):
                        head_sums(s + 3, 1 - par)
                    if q == 26 and has(s + 3):
                        token_sums(s + 3)
                    if q == 26 and has(s + 3):
                        token_mean(s + 3)
                        center_heads(s + 3, 1 - par)
                    if q == 26 and has(s + 3):
                        head_offsets(s + 3)
                    if q == 27 and has(s + 3):
                        square_offsets(s + 3)
                        head_squares(s + 3)
                    if q == 28 and has(s + 3):
                        token_parts(s + 3)
                    if q == 30 and has(s + 2):
                        statistics(s + 2, 0)
                    if q == 31 and has(s + 2):
                        statistics(s + 2, 1)
                    if q == 31 and has(s + 2):
                        aggregate(s + 2)
                    if q == 2 and has(s + 1):
                        scale_again(s + 1)
                    if q == 7 and has(s + 1):
                        split_lo(s + 1, 1 - par, 0)
                    if q == 10 and has(s + 1):
                        split_lo(s + 1, 1 - par, 1)
                    if q == 13 and has(s + 1):
                        add_gate_bias(s + 1)
                    if q == 14 and has(s + 1):
                        add_hi_part(s + 1)
                        top_values(s + 1)
                    if q == 15 and has(s + 1):
                        top_gap(s + 1)
                    if q == 14 and has(s + 1):
                        top_places(s + 1)
                    if q == 15 and has(s + 1):
                        places_as_floats(s + 1)
                    if q == 16 and has(s + 1):
                        mark_experts(s + 1)
                    if q == 18 and has(s + 1):
                        gate_sum(s + 1)
                    if q == 19 and has(s + 1):
                        first_weight(s + 1)
                    if q == 19 and has(s + 1):
                        second_weight(s + 1)
                    if q == 20 and has(s + 1):
                        weigh_marks(s + 1)
                    if q == 22 and has(s + 1):
                        sum_gates(s + 1)
                    if q == 8 and has(s - 1):
                        add_ffn(s - 1, 1 - par)
                    if q == 10 and has(s - 1):
                        sums_last(s - 1)
                    if q == 12 and has(s - 1):
                        divide_last(s - 1)
                    if q == 15 and has(s - 1):
                        squares_last(s - 1)
                    if q == 16 and has(s - 1):
                        invert_last(s - 1)
                    if q == 18 and has(s - 1):
                        scale_last(s - 1)

            pipeline(dve, step)

        @block.tensor
        def _(pe):
            pe.wait_ge(embed_in, 5 * 16)
            pe.wait_ge(sparse_in, 3 * 16)
            pe.wait_ge(embed_weights, 3)
            pe.wait_ge(ones_ready, 2)

            def embed_patches(k, par):
                pe.wait_ge(loaded, 16 * (k + 1))
                wait(pe, g_copied, 2 * (k - 2))
                wait(pe, ysum_ready, k - 3)
                for j in range(TT):
                    last = nc.tensor.matmul(pf[:, j * P:(j + 1) * P], xin[par][:, j * P:(j + 1) * P],
                                            wt[:, :], start=True, stop=True)
                last.then_inc(embedded, 1)

            def turn_tokens(k):
                pe.wait_ge(hcen_ready, k + 1)
                wait(pe, osc_ready, k)
                for j in range(TT):
                    last = nc.tensor.transpose(pa[:, j * P:(j + 1) * P], hcen[:, j * P:(j + 1) * P], eye[:, :])
                last.then_inc(ht_turned, 1)

            def gram(k):
                pe.wait_ge(n_ready, k + 1)
                pe.wait_ge(ht_copied, k + 1)
                for t in range(T):
                    last = nc.tensor.matmul(pa[0:C + 1, 0:C + 1], naug[:, t, :], naug[:, t, :],
                                            start=(t == 0), stop=(t == T - 1))
                last.then_inc(m_done, 1)

            def times_v(k):
                pe.wait_ge(m_copied, k + 1)
                nc.tensor.matmul(pa[0:C + 1, 128:128 + C], maug[:, :], vaug[:, :], start=True,
                                 stop=True).then_inc(t_done, 1)

            def times_k(k):
                pe.wait_ge(t_copied, k + 1)
                nc.tensor.matmul(pa[:, 256:256 + C], kaug[:, :], tm[:, :], start=True,
                                 stop=True).then_inc(kv_done, 1)

            def attention(k):
                pe.wait_ge(am_ready, k + 1)
                pe.wait_ge(am0_ready, k + 1)
                for j in range(TT):
                    last = nc.tensor.matmul(pa[:, j * P:(j + 1) * P], ht[:, j * P:(j + 1) * P], am[:, :],
                                            start=True, stop=True)
                last.then_inc(attended, 1)

            def turn_x(k):
                pe.wait_ge(xn_ready, k + 1)
                wait(pe, g_copied, 2 * k)
                for j in range(TT):
                    last = nc.tensor.transpose(pb[:, j * P:(j + 1) * P], xn[:, j * P:(j + 1) * P], eye[:, :])
                last.then_inc(x_turned, 1)

            def gate_logits(k, par):
                pe.wait_ge(lo_ready, 2 * k + 2)
                for b in range(T):
                    last = nc.tensor.matmul(pb[:, 2 * b * NE:2 * (b + 1) * NE], xs[par][:, columns(b)],
                                            gwr[:, :], start=True, stop=True)
                last.then_inc(logits_done, 1)

            def turn_gates(k, half):
                pe.wait_ge(spread_ready, k + 1)
                if half == 0:
                    pe.wait_ge(logit_ready, k + 1)
                else:
                    pe.wait_ge(h_ready, min(k + 3, B) if isinstance(k, int) else k + 3)
                    wait(pe, ysum_ready, k - 1)
                for j in range(TT):
                    b = 2 * j + half
                    last = nc.tensor.transpose((pb, pf)[half][:, j * P:(j + 1) * P],
                                               spread[:, b * P:(b + 1) * P], eye[:, :])
                last.then_inc(g_turned, 1)

            def hidden(s, par, q):
                c = q % CHUNKS
                if on_pool(q):
                    wait(pe, relu_done, STEP * s + q - SRING + 1)
                else:
                    wait(pe, gated_dve, DVE_STEP * s + (dve_gated(q - SRING) if q >= SRING else
                                                        dve_gated(q - SRING + STEP) - DVE_STEP))
                if q % CHUNKS == 0:
                    pe.wait_ge(lo_ready, 2 * s + q // CHUNKS + 1)
                nc.tensor.matmul(ps[q % SRING][:, :], w1h[:, c * P:(c + 1) * P], xs[par][:, tile_of(q)],
                                 start=True, stop=False)
                nc.tensor.matmul(ps[q % SRING][:, :], w1l[:, c * P:(c + 1) * P], xs[par][:, tile_of(q)],
                                 start=False, stop=True).then_inc(s_done, 1)

            def combine(s, par, q):
                first, final = q % CHUNKS == 0, q % CHUNKS == CHUNKS - 2
                pe.wait_ge(gated_dve, DVE_STEP * s + dve_gated(q + 1))
                if on_pool(q + 1):
                    pe.wait_ge(gated_pool, POOL_STEP * s + pool_gated(q + 1))
                if first:
                    wait(pe, y_copied, TILES * s + q // CHUNKS)
                for half in range(2):
                    c = (q + half) % CHUNKS
                    last = nc.tensor.matmul(py[half * C:(half + 1) * C, :], w2s[:, c * C:(c + 1) * C],
                                            hg[(q + half) % GRING][:, :], start=first, stop=final,
                                            skip_group_check=True)
                if first:
                    for half in range(2):
                        at = half * (W // 2)
                        tokens = tile_of(q).start + at
                        last = nc.tensor.matmul(py[half * C:(half + 1) * C, at:at + W // 2], b2x[:, :],
                                                gt[par][:, tokens:tokens + W // 2], start=False, stop=False,
                                                skip_group_check=True)
                last.then_inc(y_pairs, 1)

            def tokens_again(k):
                pe.wait_ge(y_added, k + 1)
                pe.wait_ge(g_copied, min(2 * k + 4, 2 * B) if isinstance(k, int) else 2 * k + 4)
                for j in range(TT):
                    last = nc.tensor.transpose(pf[:, j * P:(j + 1) * P], yt[:, j * P:(j + 1) * P], eye[:, :])
                last.then_inc(f_done, 1)

            def step(s, par):
                for q in range(STEP):
                    if has(s):
                        hidden(s, par, q)
                    if q == GROUP - 1 and has(s - 1):
                        for pair in range(STEP - GROUP, STEP, 2):
                            combine(s - 1, 1 - par, pair)
                    if q % GROUP == GROUP - 1 and q >= GROUP and has(s):
                        for pair in range(q + 1 - 2 * GROUP, q + 1 - GROUP, 2):
                            combine(s, par, pair)
                    if q == 7 and has(s - 1):
                        tokens_again(s - 1)
                    if q == 7 and has(s + 1):
                        turn_x(s + 1)
                    if q == 9 and isinstance(s, int) and s == -1:
                        pe.wait_ge(ffn_in, 3 * 16)
                        pe.wait_ge(ffn_weights, 2)
                    if q == 14 and has(s + 1):
                        gate_logits(s + 1, 1 - par)
                    if q == 11 and has(s + 2):
                        turn_tokens(s + 2)
                    if q == 16 and has(s + 2):
                        gram(s + 2)
                    if q == 20 and has(s + 2):
                        times_v(s + 2)
                    if q == 22 and has(s + 2):
                        times_k(s + 2)
                    if q == 25 and has(s + 3):
                        embed_patches(s + 3, 1 - par)
                    if q == 28 and has(s + 2):
                        attention(s + 2)
                    if q == 27 and has(s + 1):
                        turn_gates(s + 1, 0)
                        turn_gates(s + 1, 1)

            pipeline(pe, step)


def kernel(x, L0_tok_W, L0_tok_b, L0_tok_pos_embed, L0_attn_kln_weight, L0_attn_kln_bias,
           L0_attn_vln_weight, L0_attn_vln_bias, L0_ffn_gate_w, L0_ffn_gate_b, L0_ffn_w1, L0_ffn_b1,
           L0_ffn_w2, L0_ffn_b2, L0_ffn_gamma, L0_ffn_beta):
    import numpy as np
    import concourse.bacc as bacc
    from concourse.bass_utils import run_bass_kernel_spmd

    patches = np.asarray(x).reshape(B, 16, 8, 64, 8).transpose(0, 2, 4, 1, 3).reshape(B, C, P, TT, 2)
    w1 = np.asarray(L0_ffn_w1).reshape(NE, C, CHUNKS, UN).transpose(1, 2, 0, 3).reshape(C, CHUNKS * P)
    w2 = np.asarray(L0_ffn_w2).reshape(NE, CHUNKS, UN, C).transpose(0, 2, 1, 3).reshape(P, CHUNKS * C)
    b1 = np.asarray(L0_ffn_b1).reshape(NE, CHUNKS, UN).transpose(0, 2, 1).reshape(P, CHUNKS)
    k_w, v_w, k_b, v_b = (np.asarray(v).reshape(C) for v in (
        L0_attn_kln_weight, L0_attn_vln_weight, L0_attn_kln_bias, L0_attn_vln_bias))
    gate_w = np.asarray(L0_ffn_gate_w)
    head = np.arange(P) // HD
    fixed = np.zeros((P, 2 * P + NE + T), np.float32)
    fixed[:, :P] = np.eye(P)
    fixed[:, P:2 * P] = (head[:, None] == head[None, :]).astype(np.float32) / np.float32(N)
    fixed[:, 2 * P:2 * P + NE] = np.arange(NE)
    fixed[:, 2 * P + NE:] = np.e
    arrays = {
        "patches": patches.transpose(0, 4, 1, 3, 2).reshape(B, P, W),
        "tok_w": np.asarray(L0_tok_W).T,
        "pos": np.asarray(L0_tok_pos_embed).reshape(P, T * C),
        "vectors": np.concatenate([np.asarray(v) for v in (L0_tok_b, L0_ffn_gamma, L0_ffn_beta, L0_ffn_gate_b)]),
        "kv_weight": np.stack([k_w, v_w], axis=1),
        "kv_bias": np.concatenate([k_b, k_b, v_b]),
        "per_row": np.concatenate([np.concatenate([gate_w, gate_w]), b1], axis=1),
        "w1": np.concatenate([w1, w1]),
        "w2": w2,
        "b2": L0_ffn_b2,
        "fixed": fixed,
    }
    nc = bacc.Bacc("TRN2", target_bir_lowering=False, num_devices=1)
    given, args = {}, []
    for name, a in arrays.items():
        a = np.ascontiguousarray(a)
        given[f"in_{name}"] = a
        args.append(nc.dram_tensor(f"in_{name}", a.shape, mybir.dt.from_np(a.dtype),
                                   kind="ExternalInput").ap())
    out = nc.dram_tensor("out", (B, P, T * C), F32, kind="ExternalOutput").ap()
    tower(nc, *args, out)
    r = run_bass_kernel_spmd(nc, [given], core_ids=[0])
    return r.results[0]["out"].reshape(B, N, C)
```
